# Optimizing a Trainium2 kernel written in Bass

```python
import numpy as np
import jax
import jax.numpy as jnp

def _softmax(x, axis=-1):
    return jax.nn.softmax(x, axis=axis)

def _gelu(x):
    return jax.nn.gelu(x, approximate=True)

def _silu(x):
    return jax.nn.silu(x)

def _sigmoid(x):
    return jax.nn.sigmoid(x)

def _layernorm(x, axis=-1, eps=1e-05):
    m = jnp.mean(x, axis=axis, keepdims=True)
    v = jnp.var(x, axis=axis, keepdims=True)
    return (x - m) / jnp.sqrt(v + eps)

def _scatter_add(tgt, idx, src, axis=0):
    return tgt.at[idx].add(src)

def _segment_sum(src, seg, n):
    return jax.ops.segment_sum(src, seg, n)
kernel_name = 'mk_macaron_d1_jaxref_r8_4f13b4'

def setup_inputs(seed: int=0):
    np.random.seed(seed)
    _w = jnp.asarray

    def _L0_attn_setup():
        import jax, jax.numpy as jnp
        import numpy as np
        E = 128
        H = 16
        D = E // H
        B = 2
        N = 1024
        CHUNK = 128
        LAYER_IDX = 0
        NUM_LAYERS = 12
        EPS = 1e-05

        def _build_slopes(n):

            def po2(m):
                start = 2.0 ** (-2.0 ** (-(np.log2(m) - 3)))
                return [start * start ** i for i in range(m)]
            if np.log2(n).is_integer():
                return po2(n)
            closest = 2 ** int(np.floor(np.log2(n)))
            return po2(closest) + _build_slopes(2 * closest)[0::2][:n - closest]

        def _slope_rate():
            s = np.array(_build_slopes(H), dtype=np.float32)
            s = s * (1.0 - LAYER_IDX / (NUM_LAYERS - 1) + 1e-05)
            return jnp.asarray(s)

        def lightning_attn(q, k, v, s):
            b, h, n, d = q.shape
            nc = n // CHUNK
            idx = jnp.arange(CHUNK, dtype=q.dtype)
            diff = idx[:, None] - idx[None, :]
            mask = jnp.where(diff >= 0, jnp.exp(-s[:, None, None] * diff), 0.0)
            lam_q = jnp.exp(-s[:, None] * (idx + 1.0))
            lam_k = jnp.exp(-s[:, None] * (CHUNK - 1.0 - idx))
            lam_c = jnp.exp(-s * CHUNK)

            def to_chunks(t):
                return t.reshape(b, h, nc, CHUNK, d).transpose(2, 0, 1, 3, 4)
            qc, kc, vc = (to_chunks(q), to_chunks(k), to_chunks(v))

            def step(kv, xs):
                qi, ki, vi = xs
                scores = jnp.einsum('bhid,bhjd->bhij', qi, ki) * mask
                o = jnp.einsum('bhij,bhjd->bhid', scores, vi)
                o = o + lam_q[:, :, None] * jnp.einsum('bhid,bhde->bhie', qi, kv)
                kv = lam_c[:, None, None] * kv + jnp.einsum('bhid,bhie->bhde', ki * lam_k[:, :, None], vi)
                return (kv, o)
            kv0 = jnp.zeros((b, h, d, d), q.dtype)
            _, o = jax.lax.scan(step, kv0, (qc, kc, vc))
            return o.transpose(1, 2, 0, 3, 4).reshape(b, h, n, d)
        key = jax.random.key(seed)
        ks = jax.random.split(key, 8)
        sc = 1.0 / np.sqrt(E)
        return {'x': jax.random.normal(ks[0], (B, N, E), jnp.float32), 'Wq': jax.random.normal(ks[1], (E, E), jnp.float32) * sc, 'Wk': jax.random.normal(ks[2], (E, E), jnp.float32) * sc, 'Wv': jax.random.normal(ks[3], (E, E), jnp.float32) * sc, 'Wo': jax.random.normal(ks[4], (E, E), jnp.float32) * sc, 'gamma': jnp.ones((E,), jnp.float32), 'beta': jnp.zeros((E,), jnp.float32), 'Wg1': jax.random.normal(ks[5], (E, D), jnp.float32) * sc, 'Wg2': jax.random.normal(ks[6], (D, E), jnp.float32) * (1.0 / np.sqrt(D))}
    _L0_attn_in = _L0_attn_setup()

    def _L0_ffn_setup():
        import jax, jax.numpy as jnp
        import numpy as np
        D_MODEL, D_FF, N_EXP = (128, 512, 8)
        key = jax.random.key(seed)
        ks = jax.random.split(key, 8)
        s = lambda fan_in: 1.0 / np.sqrt(fan_in)
        x = jax.random.normal(ks[0], (4, 256, D_MODEL), dtype=jnp.float32)
        Wr = jax.random.uniform(ks[1], (N_EXP, D_MODEL), jnp.float32, -s(D_MODEL), s(D_MODEL))
        br = jax.random.uniform(ks[2], (N_EXP,), jnp.float32, -s(D_MODEL), s(D_MODEL))
        W1 = jax.random.uniform(ks[3], (N_EXP, D_FF, D_MODEL), jnp.float32, -s(D_MODEL), s(D_MODEL))
        b1 = jax.random.uniform(ks[4], (N_EXP, D_FF), jnp.float32, -s(D_MODEL), s(D_MODEL))
        W2 = jax.random.uniform(ks[5], (N_EXP, D_MODEL, D_FF), jnp.float32, -s(D_FF), s(D_FF))
        b2 = jax.random.uniform(ks[6], (N_EXP, D_MODEL), jnp.float32, -s(D_FF), s(D_FF))
        return {'x': x, 'Wr': Wr, 'br': br, 'W1': W1, 'b1': b1, 'W2': W2, 'b2': b2}
    _L0_ffn_in = _L0_ffn_setup()
    _d = {'L0_attn_x': _L0_attn_in['x'], 'L0_attn_Wq': _L0_attn_in['Wq'], 'L0_attn_Wk': _L0_attn_in['Wk'], 'L0_attn_Wv': _L0_attn_in['Wv'], 'L0_attn_Wo': _L0_attn_in['Wo'], 'L0_attn_gamma': _L0_attn_in['gamma'], 'L0_attn_beta': _L0_attn_in['beta'], 'L0_attn_Wg1': _L0_attn_in['Wg1'], 'L0_attn_Wg2': _L0_attn_in['Wg2'], 'L0_ffn_Wr': _L0_ffn_in['Wr'], 'L0_ffn_br': _L0_ffn_in['br'], 'L0_ffn_W1': _L0_ffn_in['W1'], 'L0_ffn_b1': _L0_ffn_in['b1'], 'L0_ffn_W2': _L0_ffn_in['W2'], 'L0_ffn_b2': _L0_ffn_in['b2']}
    _x0 = _d['L0_attn_x']
    _d['L0_attn_x'] = jax.random.normal(jax.random.fold_in(jax.random.key(seed), 1), (4, 1024, 128), dtype=_x0.dtype)
    del _x0
    return _d

def reference(L0_attn_x, L0_attn_Wq, L0_attn_Wk, L0_attn_Wv, L0_attn_Wo, L0_attn_gamma, L0_attn_beta, L0_attn_Wg1, L0_attn_Wg2, L0_ffn_Wr, L0_ffn_br, L0_ffn_W1, L0_ffn_b1, L0_ffn_W2, L0_ffn_b2):

    def _L0_attn_ref(x, Wq, Wk, Wv, Wo, gamma, beta, Wg1, Wg2):
        import jax, jax.numpy as jnp
        import numpy as np
        E = 128
        H = 16
        D = E // H
        B = 2
        N = 1024
        CHUNK = 128
        LAYER_IDX = 0
        NUM_LAYERS = 12
        EPS = 1e-05

        def _build_slopes(n):

            def po2(m):
                start = 2.0 ** (-2.0 ** (-(np.log2(m) - 3)))
                return [start * start ** i for i in range(m)]
            if np.log2(n).is_integer():
                return po2(n)
            closest = 2 ** int(np.floor(np.log2(n)))
            return po2(closest) + _build_slopes(2 * closest)[0::2][:n - closest]

        def _slope_rate():
            s = np.array(_build_slopes(H), dtype=np.float32)
            s = s * (1.0 - LAYER_IDX / (NUM_LAYERS - 1) + 1e-05)
            return jnp.asarray(s)

        def lightning_attn(q, k, v, s):
            b, h, n, d = q.shape
            nc = n // CHUNK
            idx = jnp.arange(CHUNK, dtype=q.dtype)
            diff = idx[:, None] - idx[None, :]
            mask = jnp.where(diff >= 0, jnp.exp(-s[:, None, None] * diff), 0.0)
            lam_q = jnp.exp(-s[:, None] * (idx + 1.0))
            lam_k = jnp.exp(-s[:, None] * (CHUNK - 1.0 - idx))
            lam_c = jnp.exp(-s * CHUNK)

            def to_chunks(t):
                return t.reshape(b, h, nc, CHUNK, d).transpose(2, 0, 1, 3, 4)
            qc, kc, vc = (to_chunks(q), to_chunks(k), to_chunks(v))

            def step(kv, xs):
                qi, ki, vi = xs
                scores = jnp.einsum('bhid,bhjd->bhij', qi, ki) * mask
                o = jnp.einsum('bhij,bhjd->bhid', scores, vi)
                o = o + lam_q[:, :, None] * jnp.einsum('bhid,bhde->bhie', qi, kv)
                kv = lam_c[:, None, None] * kv + jnp.einsum('bhid,bhie->bhde', ki * lam_k[:, :, None], vi)
                return (kv, o)
            kv0 = jnp.zeros((b, h, d, d), q.dtype)
            _, o = jax.lax.scan(step, kv0, (qc, kc, vc))
            return o.transpose(1, 2, 0, 3, 4).reshape(b, h, n, d)
        b, n, e = x.shape
        s = _slope_rate()
        silu = jax.nn.silu
        q = silu(x @ Wq)
        k = silu(x @ Wk)
        v = silu(x @ Wv)
        split = lambda t: t.reshape(b, n, H, D).transpose(0, 2, 1, 3)
        o = lightning_attn(split(q), split(k), split(v), s)
        o = o.transpose(0, 2, 1, 3).reshape(b, n, e)
        mu = jnp.mean(o, axis=-1, keepdims=True)
        var = jnp.var(o, axis=-1, keepdims=True)
        o = (o - mu) * jax.lax.rsqrt(var + EPS) * gamma + beta
        gate = jax.nn.sigmoid(x @ Wg1 @ Wg2)
        return o * gate @ Wo

    def _L0_ffn_ref(x, Wr, br, W1, b1, W2, b2):
        import jax, jax.numpy as jnp
        import numpy as np
        D_MODEL, D_FF, N_EXP = (128, 512, 8)
        B, S, D = x.shape
        xf = x.reshape(-1, D)
        logits = xf @ Wr.T + br
        expert_idx = jnp.argmax(logits, axis=-1)
        h = jax.nn.relu(jnp.einsum('td,efd->etf', xf, W1) + b1[:, None, :])
        y = jnp.einsum('etf,edf->etd', h, W2) + b2[:, None, :]
        out = y[expert_idx, jnp.arange(xf.shape[0])]
        return out.reshape(B, S, D)
    x = L0_attn_x
    x = x + 0.5 * _L0_ffn_ref(_layernorm(x, axis=-1), L0_ffn_Wr, L0_ffn_br, L0_ffn_W1, L0_ffn_b1, L0_ffn_W2, L0_ffn_b2)
    x = x + _L0_attn_ref(_layernorm(x, axis=-1), L0_attn_Wq, L0_attn_Wk, L0_attn_Wv, L0_attn_Wo, L0_attn_gamma, L0_attn_beta, L0_attn_Wg1, L0_attn_Wg2)
    x = x + 0.5 * _L0_ffn_ref(_layernorm(x, axis=-1), L0_ffn_Wr, L0_ffn_br, L0_ffn_W1, L0_ffn_b1, L0_ffn_W2, L0_ffn_b2)
    return x

_drawn_inputs = setup_inputs


def setup_inputs(seed=0):
    import zlib

    import numpy as np

    out = dict(_drawn_inputs(seed))
    spreads = {'L0_attn_gamma': (1.0, 0.2), 'L0_attn_beta': (0.0, 0.1)}
    factors = {'L0_ffn_b1': 2.772}
    for name, (base, spread) in spreads.items():
        noise = np.random.default_rng([zlib.crc32(name.encode()), seed]).standard_normal(out[name].shape)
        drawn = base * np.exp(spread * noise) if base else spread * noise
        out[name] = jnp.asarray(drawn.astype(out[name].dtype))
    for name, factor in factors.items():
        out[name] = (out[name] * factor).astype(out[name].dtype)
    return out
```

```python
from collections import namedtuple
from contextlib import ExitStack

import numpy as np

import concourse.bass as bass
from concourse import mybir

F32 = mybir.dt.float32
BF16 = mybir.dt.bfloat16
I32 = mybir.dt.int32
ALU = mybir.AluOpType
ACT = mybir.ActivationFunctionType
AX_X = mybir.AxisListType.X

P = 128
BATCH, SEQ, D = 4, 1024, 128
STEPS = SEQ // P
TOKEN_TILES = BATCH * STEPS
EXPERTS, FF = 8, 512
FB = FF // P
SLOT_TILES = TOKEN_TILES + EXPERTS - 1
HEADS = 16
HD = D // HEADS
PAIRS = HEADS // 2
UH = HD * HD
UW = HEADS * UH
EPS = 1e-5
ROUND = 1.5 * 2.0 ** 23
RSQRT_MAGIC = float(0x5F3759DF)

CONST = {}
_at = 0
for _name, _width in (("ident", P), ("carry_mask", P), ("decay_q", P), ("decay_k", P), ("decay_c", 1),
                      ("upper", P), ("ones", P), ("not_first", EXPERTS * TOKEN_TILES),
                      ("prefer", EXPERTS), ("slot_tile", SLOT_TILES)):
    CONST[_name] = (_at, _width)
    _at += _width
CONST_W = _at

Step = namedtuple("Step", "n half par")


def step(k, it=0):
    return Step(2 * it + k, it + k // 2, k % 2)


def wait(eng, sem, value):
    if isinstance(value, int) and value <= 0:
        return
    eng.wait_ge(sem, value)


def rolled(eng, body, first, loop_from, loop_to, end):
    for k in range(first, loop_from):
        body(k)
    with eng.Fori(0, (loop_to - loop_from) // 2) as it:
        for k in (loop_from, loop_from + 1):
            body(k, it)
    for k in range(loop_from + (loop_to - loop_from) // 2 * 2, end):
        body(k)


class Chain:

    def __init__(self, eng, sem, per):
        self.eng, self.sem, self.per = eng, sem, per

    def begin(self, n):
        self.base, self.k = n * self.per, 0

    def link(self, ins):
        self.k += 1
        ins.then_inc(self.sem, 1)
        self.eng.wait_ge(self.sem, self.base + self.k)

    def end(self):
        assert self.k == self.per


def build(nc, x, w1t, b1, w2t, b2, wrt, br, wqkv, wg1t, wg2, wo, gamma, beta, decay, const, out):
    with ExitStack() as ctx:
        def sb(name, shape, dt=F32):
            return ctx.enter_context(nc.sbuf_tensor(name, shape, dt))

        def pb(name, shape=(P, 512)):
            return ctx.enter_context(nc.psum_tensor(name, list(shape), F32))

        def sem(name):
            return ctx.enter_context(nc.semaphore(name))

        slots_in = nc.dram_tensor("slots_in", (SLOT_TILES * P, D), F32, kind="Internal").ap()
        slots_out = nc.dram_tensor("slots_out", (SLOT_TILES * P, D), F32, kind="Internal").ap()
        slots_in_v = slots_in.rearrange("(t p) d -> p t d", p=P)
        slots_out_v = slots_out.rearrange("(t p) d -> p t d", p=P)

        res = sb("res", [P, TOKEN_TILES * D])
        normed = sb("normed", [P, TOKEN_TILES * D])
        slot_y = sb("slot_y", [P, SLOT_TILES * D])
        w1_sb = sb("w1_sb", [P, EXPERTS * FF])
        w2_sb = sb("w2_sb", [P, EXPERTS * FF])
        b1_sb = sb("b1_sb", [P, EXPERTS * FF])
        b2_sb = sb("b2_sb", [P, EXPERTS * D])
        decay_sb = sb("decay_sb", [P, HEADS * P])
        const_sb = sb("const_sb", [P, CONST_W])
        wr_sb = sb("wr_sb", [P, EXPERTS])
        br_sb = sb("br_sb", [P, EXPERTS])
        wqkv_sb = sb("wqkv_sb", [P, 3 * D])
        wo_sb = sb("wo_sb", [P, D])
        wg1_sb = sb("wg1_sb", [HD, D])
        wg2_sb = sb("wg2_sb", [HD, D])
        wg_sb = sb("wg_sb", [P, D])
        gb_sb = sb("gb_sb", [P, 2])
        upper_bf = sb("upper_bf", [P, P], BF16)
        ones_bf = sb("ones_bf", [P, P], BF16)

        back = [sb(f"back{i}", [P, BATCH * D]) for i in range(2)]
        xn = [sb(f"xn{i}", [P, BATCH * D]) for i in range(2)]
        xnT = [sb(f"xnT{i}", [P, BATCH * P]) for i in range(2)]
        rn = [sb(f"rn{i}", [P, BATCH * D]) for i in range(2)]
        rnT = [sb(f"rnT{i}", [P, BATCH * P]) for i in range(2)]
        qkv = [sb(f"qkv{i}", [P, BATCH * 3 * D]) for i in range(2)]
        gateT = [sb(f"gateT{i}", [P, BATCH * P]) for i in range(2)]
        outer = [sb("outer", [P, BATCH * UW]), slot_y[:, 0:BATCH * UW]]
        kd = [sb(f"kd{i}", [P, BATCH * D]) for i in range(2)]
        qdT = [sb(f"qdT{i}", [P, BATCH * P]) for i in range(2)]
        qS = [sb(f"qS{i}", [P, 512]) for i in range(2)]
        o_in = sb("o_in", [P, BATCH * D])
        o_all = sb("o_all", [P, BATCH * D])
        o_n = sb("o_n", [P, BATCH * D])
        o_nT = sb("o_nT", [P, BATCH * P])
        o_gT = sb("o_gT", [P, BATCH * P])
        carry = sb("carry", [P, BATCH * D])
        carry_new = sb("carry_new", [P, BATCH * D])
        h_pre, h_T = kd, qdT
        slot_x = [o_all[:, i * D:(i + 1) * D] for i in range(2)]
        slotT = [o_all[:, (2 + i) * D:(3 + i) * D] for i in range(2)]

        logits = sb("logits", [P, TOKEN_TILES * EXPERTS])
        onehot = sb("onehot", [P, TOKEN_TILES * EXPERTS])
        onehot_bf = sb("onehot_bf", [P, TOKEN_TILES * EXPERTS], BF16)
        total = sb("total", [P, TOKEN_TILES * EXPERTS])
        upto = sb("upto", [P, TOKEN_TILES * EXPERTS])
        place = sb("place", [P, TOKEN_TILES * EXPERTS])
        pick = place
        best = sb("best", [P, TOKEN_TILES])
        tiles_e = sb("tiles_e", [P, EXPERTS])
        ends_e = sb("ends_e", [P, EXPERTS])
        base_e = sb("base_e", [P, EXPERTS])
        ended = sb("ended", [1, SLOT_TILES * EXPERTS])
        slot_of_f = sb("slot_of_f", [P, TOKEN_TILES])
        owner_f = sb("owner_f", [1, SLOT_TILES])
        owner = [sb(f"owner{i}", [1, SLOT_TILES], I32) for i in range(2)]
        slot_of = [sb(f"slot_of{i}", [P, TOKEN_TILES], I32) for i in range(2)]

        def stats_bufs(name):
            return dict(st=sb(f"{name}_st", [P, BATCH, 6]), mean2=sb(f"{name}_mean2", [P, BATCH]),
                        v=sb(f"{name}_v", [P, BATCH]), y=sb(f"{name}_y", [P, BATCH]),
                        t=sb(f"{name}_t", [P, BATCH]), u=sb(f"{name}_u", [P, BATCH]),
                        rstd=[sb(f"{name}_rstd{i}", [P, BATCH]) for i in range(2)],
                        shift=[sb(f"{name}_shift{i}", [P, BATCH]) for i in range(2)])

        ln_route, ln_attn, ln_out = stats_bufs("lr"), stats_bufs("la"), stats_bufs("lo")

        bank = [pb(f"bank{i}") for i in range(8)]

        def cst(name, rows=P):
            a, w = CONST[name]
            return const_sb[0:rows, a:a + w]

        ident = cst("ident")
        per_batch = lambda ap, w=D: ap.rearrange("p (b d) -> p b d", b=BATCH)
        of_step = lambda t, s, w=BATCH * D: t[:, bass.ds(s.n * w, w)]

        x_loaded = [sem(f"x_loaded{i}") for i in range(2)]
        const_loaded, decay_loaded = sem("const_loaded"), sem("decay_loaded")
        router_loaded, attn_w_loaded, expert_w_loaded = sem("router_loaded"), sem("attn_w_loaded"), sem("expert_w_loaded")
        zeroed, slots_cleared = sem("zeroed"), sem("slots_cleared")
        bf_ready, wg_ready, wg_copied = sem("bf_ready"), sem("wg_ready"), sem("wg_copied")
        two = lambda name: [sem(f"{name}{i}") for i in range(2)]
        ln_done, rn_done, rnT_ready, rnT_copied = two("ln_done"), two("rn_done"), two("rnT_ready"), two("rnT_copied")
        logits_ready, logits_added, rows_kept = two("logits_ready"), two("logits_added"), two("rows_kept")
        ln_chain = two("ln_chain")
        slots_chain = two("slots_chain")
        route_chain, onehot_ready, counts_ready, slots_known, owners_known = (
            two("route_chain"), two("onehot_ready"), two("counts_ready"), two("slots_known"), two("owners_known"))
        rows_sorted = two("rows_sorted")
        slot_loaded = [two(f"slot_loaded{i}_") for i in range(2)]
        slotT_ready, slotT_copied, up_done, b1_added, hT_ready, hT_copied, down_done, b2_added, y_stored = (
            two("slotT_ready"), two("slotT_copied"), two("up_done"), two("b1_added"), two("hT_ready"),
            two("hT_copied"), two("down_done"), two("b2_added"), two("y_stored"))
        fetched = [two(f"fetched{i}_") for i in range(2)]
        mixed_in, la_chain, la_done, xn_done, xnT_ready, xnT_copied = (
            sem("mixed_in"), sem("la_chain"), sem("la_done"), sem("xn_done"), sem("xnT_ready"), sem("xnT_copied"))
        qkv_ready, qkv_done, gate_ready, gate_done = sem("qkv_ready"), sem("qkv_done"), sem("gate_ready"), sem("gate_done")
        outer_done, kd_done, qT_ready, qdT_done = sem("outer_done"), sem("kd_done"), sem("qT_ready"), sem("qdT_done")
        state_ready, qS_done, o_in_done = sem("state_ready"), sem("qS_done"), sem("o_in_done")
        inter_ready, o_done, delta_ready, delta_masked, carry_done = (
            sem("inter_ready"), sem("o_done"), sem("delta_ready"), sem("delta_masked"), sem("carry_done"))
        lo_chain, lo_done, on_done, onT_ready, onT_copied, gated, wo_ready, res_done = (
            sem("lo_chain"), sem("lo_done"), sem("on_done"), sem("onT_ready"), sem("onT_copied"), sem("gated"),
            sem("wo_ready"), sem("res_done"))
        final_done, out_stored = sem("final_done"), sem("out_stored")

        block = ctx.enter_context(nc.Block())

        @block.sync
        def _(sp):
            x_v = x.rearrange("(b c p) d -> p c b d", b=BATCH, p=P)
            res_v = res[:, :].rearrange("p (c b d) -> p c b d", c=STEPS, b=BATCH)
            half = STEPS // 2
            for b in range(BATCH):
                sp.dma_start(res_v[:, 0:half, b, :], x_v[:, 0:half, b, :]).then_inc(x_loaded[0], 16)
            sp.dma_start(const_sb[:, :], const).then_inc(const_loaded, 16)
            for b in range(BATCH):
                sp.dma_start(res_v[:, half:, b, :], x_v[:, half:, b, :]).then_inc(x_loaded[1], 16)
            sp.wait_ge(zeroed, 1)
            sp.dma_start(slots_in_v, slot_y[:, :].rearrange("p (t d) -> p t d", d=D)).then_inc(slots_cleared, 16)

            def experts(layer):
                def load(s):
                    wait(sp, slotT_ready[layer], s.n - 1)
                    sp.dma_start(slot_x[s.par][:, :], slots_in[bass.ds(s.n * P, P), :]).then_inc(slot_loaded[layer][s.par], 16)

                def store(t):
                    sp.wait_ge(b2_added[layer], t + 1)
                    sp.dma_start(slots_out[bass.ds(t * P, P), :], slot_y[:, bass.ds(t * D, D)]).then_inc(y_stored[layer], 16)

                sp.wait_ge(rows_sorted[layer], 16 * TOKEN_TILES)
                ahead = 5
                for t in range(ahead):
                    load(step(t))
                pairs = (SLOT_TILES - ahead) // 2
                with sp.Fori(0, pairs) as it:
                    for k in range(2):
                        load(step(k + ahead, it))
                        store(2 * it + k)
                with sp.Fori(2 * pairs, SLOT_TILES) as t:
                    store(t)

            experts(0)
            experts(1)
            out_v = out.rearrange("(b c p) d -> p c b d", b=BATCH, p=P)
            with sp.Fori(0, STEPS) as n:
                sp.wait_ge(final_done, n + 1)
                sp.dma_start(out_v[:, bass.ds(n, 1), :, :].rearrange("p c b d -> p (c b) d"),
                             res[:, bass.ds(n * BATCH * D, BATCH * D)].rearrange("p (b d) -> p b d", b=BATCH)).then_inc(out_stored, 16)
            sp.wait_ge(out_stored, 16 * STEPS)

        @block.gpsimd
        def _(pool):
            pool.memset(slot_y[:, :], 0.0).then_inc(zeroed, 1)

            def keep_rows(layer, s):
                pool.wait_ge(rn_done[layer], BATCH * (s.n + 1))
                pool.tensor_copy(of_step(normed, s), rn[s.par][:, :]).then_inc(rows_kept[layer], 1)

            def sort_rows(layer):
                pool.wait_ge(rows_kept[layer], STEPS)
                pool.wait_ge(slots_known[layer], 1)
                if layer == 0:
                    pool.wait_ge(slots_cleared, 16)
                for t in range(TOKEN_TILES):
                    pool.indirect_dma_start(
                        slots_in, bass.IndirectOffsetOnAxis(ap=slot_of[layer][:, t:t + 1], axis=0),
                        normed[:, t * D:(t + 1) * D], None).then_inc(rows_sorted[layer], 16)

            def fetch(layer, s, reader_done):
                wait(pool, fetched[layer][s.par], 16 * BATCH * s.half)
                wait(pool, reader_done, s.n - 1)
                for b in range(BATCH):
                    t = s.n * BATCH + b
                    pool.indirect_dma_start(
                        back[s.par][:, b * D:(b + 1) * D], None, slots_out,
                        bass.IndirectOffsetOnAxis(ap=slot_of[layer][:, t:t + 1], axis=0)).then_inc(fetched[layer][s.par], 16)

            def outer_products(s):
                pool.wait_ge(qkv_done, BATCH * (s.n + 1))
                wait(pool, state_ready, PAIRS * (s.n - 1))
                for b in range(BATCH):
                    for h in range(2):
                        n = HEADS // 2
                        at = b * 3 * D + h * n * HD
                        k_ = qkv[s.par][:, at + D:at + D + n * HD].unsqueeze(2).to_broadcast([P, n * HD, HD])
                        v_ = (qkv[s.par][:, at + 2 * D:at + 2 * D + n * HD].rearrange("p (h e) -> p h e", e=HD)
                              .unsqueeze(2).to_broadcast([P, n, HD, HD]))
                        u_ = outer[s.par][:, b * UW + h * n * UH:b * UW + (h + 1) * n * UH]
                        last = pool.tensor_tensor(u_.rearrange("p (h d e) -> p h d e", d=HD, e=HD),
                                                  k_.rearrange("p (h d) e -> p h d e", d=HD), v_, ALU.mult)
                last.then_inc(outer_done, 1)

            with pool.Fori(0, STEPS // 2) as it:
                for k in range(2):
                    keep_rows(0, step(k, it))
            sort_rows(0)
            pool.wait_ge(y_stored[0], 16 * SLOT_TILES)

            for k in range(-2, STEPS + 1):
                if k + 2 < STEPS:
                    fetch(0, step(k + 2), mixed_in)
                if 0 <= k + 1 < STEPS:
                    outer_products(step(k + 1))
                if k >= 1:
                    keep_rows(1, step(k - 1))
            sort_rows(1)
            pool.wait_ge(y_stored[1], 16 * SLOT_TILES)
            for k in range(STEPS):
                fetch(1, step(k), final_done)

        @block.scalar
        def _(act):
            act.dma_start(wr_sb[:, :], wrt).then_inc(router_loaded, 16)
            act.dma_start(br_sb[:, :], br.partition_broadcast(P)).then_inc(router_loaded, 16)
            act.dma_start(w1_sb[:, :], w1t).then_inc(expert_w_loaded, 16)
            act.dma_start(w2_sb[:, :], w2t).then_inc(expert_w_loaded, 16)
            act.dma_start(b1_sb[:, :], b1.partition_broadcast(P)).then_inc(expert_w_loaded, 16)
            act.dma_start(b2_sb[:, :], b2.partition_broadcast(P)).then_inc(expert_w_loaded, 16)
            for dst, src in ((wqkv_sb, wqkv), (wo_sb, wo), (wg1_sb, wg1t), (wg2_sb, wg2)):
                act.dma_start(dst[:, :], src).then_inc(attn_w_loaded, 16)
            act.dma_start(gb_sb[:, 0:1], gamma).then_inc(attn_w_loaded, 16)
            act.dma_start(gb_sb[:, 1:2], beta).then_inc(attn_w_loaded, 16)
            act.dma_start(decay_sb[:, :], decay).then_inc(decay_loaded, 16)

            def normalise(dst, src, ln, s, done):
                for b in range(BATCH):
                    nc.scalar.activation(dst[:, b * D:(b + 1) * D], src(b), ACT.Identity,
                                         bias=ln["shift"][s.par][:, b:b + 1],
                                         scale=ln["rstd"][s.par][:, b:b + 1]).then_inc(done, 1)

            def route_norm(layer, s):
                act.wait_ge(ln_done[layer], s.n + 1)
                wait(act, rnT_ready[layer], s.n - 1)
                wait(act, rows_kept[layer], s.n - 1)
                normalise(rn[s.par], lambda b: res[:, bass.ds(s.n * BATCH * D + b * D, D)], ln_route, s, rn_done[layer])

            def route_copy(layer, s):
                act.wait_ge(rnT_ready[layer], s.n + 1)
                wait(act, logits_ready[layer], s.n - 1)
                nc.scalar.activation(rnT[s.par][:, :], bank[3][:, :], ACT.Copy).then_inc(rnT_copied[layer], 1)

            def expert_layer(layer):
                def slotT_copy(t, par):
                    act.wait_ge(slotT_ready[layer], t + 1)
                    wait(act, up_done[layer], t - 1)
                    nc.scalar.activation(slotT[par][:, :], bank[par][:, 0:P], ACT.Copy).then_inc(slotT_copied[layer], 1)

                def relu_copy(t, par):
                    act.wait_ge(hT_ready[layer], t + 1)
                    wait(act, down_done[layer], t - 1)
                    nc.scalar.activation(h_T[par][:, :], bank[4 + par][:, :], ACT.Relu).then_inc(hT_copied[layer], 1)

                def copies(k, it=0):
                    if k < SLOT_TILES:
                        slotT_copy(2 * it + k, k % 2)
                    if k >= 2:
                        relu_copy(2 * it + k - 2, k % 2)

                rolled(act, copies, 0, 4, SLOT_TILES, SLOT_TILES + 2)

            def attn_norm(s):
                act.wait_ge(la_done, s.n + 1)
                wait(act, xnT_ready, s.n - 1)
                normalise(xn[s.par], lambda b: res[:, bass.ds(s.n * BATCH * D + b * D, D)], ln_attn, s, xn_done)

            def attn_front(s):
                act.wait_ge(xnT_ready, s.n + 1)
                wait(act, gate_ready, s.n - 1)
                nc.scalar.activation(xnT[s.par][:, :], bank[5][:, :], ACT.Copy).then_inc(xnT_copied, 1)
                wait(act, qS_done, PAIRS * (s.n - 1))
                wait(act, outer_done, s.n - 1)
                wait(act, delta_ready, s.n - 1)
                for b in range(BATCH):
                    act.wait_ge(qkv_ready, BATCH * s.n + b + 1)
                    nc.scalar.activation(qkv[s.par][:, b * 3 * D:(b + 1) * 3 * D], bank[3 + b % 2][:, 0:3 * D],
                                         ACT.Silu).then_inc(qkv_done, 1)
                act.wait_ge(gate_ready, s.n + 1)
                wait(act, gated, s.n - 1)
                nc.scalar.activation(gateT[s.par][:, :], bank[6][:, :], ACT.Tanh, scale=0.5).then_inc(gate_done, 1)

            def attn_out(s):
                act.wait_ge(lo_done, s.n + 1)
                wait(act, onT_ready, s.n)
                normalise(o_n, lambda b: o_all[:, b * D:(b + 1) * D], ln_out, s, on_done)
                act.wait_ge(onT_ready, s.n + 1)
                wait(act, gated, s.n)
                nc.scalar.activation(o_nT[:, :], bank[5][:, :], ACT.Identity, bias=gb_sb[:, 1:2],
                                     scale=gb_sb[:, 0:1]).then_inc(onT_copied, 1)

            def route_step(k, it=0):
                if k < STEPS:
                    route_norm(0, step(k, it))
                if k >= 1:
                    route_copy(0, step(k - 1, it))

            rolled(act, route_step, 0, 3, STEPS - 1, STEPS + 1)

            act.wait_ge(wg_ready, 1)
            nc.scalar.activation(wg_sb[:, :], bank[7][:, 0:D], ACT.Copy).then_inc(wg_copied, 1)
            expert_layer(0)

            def attention(k, it=0):
                cur = step(k, it) if 0 <= k < STEPS else None
                nxt = step(k + 1, it) if k + 1 < STEPS else None
                prv = step(k - 1, it) if k >= 1 else None
                if nxt is not None:
                    attn_norm(nxt)
                    attn_front(nxt)
                if cur is not None:
                    attn_out(cur)
                if prv is not None:
                    route_norm(1, prv)
                    route_copy(1, prv)

            act.wait_ge(attn_w_loaded, 16 * 6)
            rolled(act, attention, -1, 2, STEPS - 1, STEPS + 1)
            expert_layer(1)

        @block.vector
        def _(dve):
            LN_PER = 16

            def layer_norm_stats(ln, chain, s, src, done):
                chain.begin(s.n)
                st, mean2, v, y, t, u = ln["st"], ln["mean2"], ln["v"], ln["y"], ln["t"], ln["u"]
                for b in range(BATCH):
                    last = nc.vector.bn_stats(st[:, b, :], src(b))
                chain.link(last)
                nc.vector.tensor_tensor(mean2[:, :], st[:, :, 1], st[:, :, 4], ALU.add)
                nc.vector.tensor_tensor(v[:, :], st[:, :, 2], st[:, :, 5], ALU.add)
                chain.link(nc.vector.tensor_tensor(t[:, :], st[:, :, 1], st[:, :, 4], ALU.subtract))
                chain.link(nc.vector.tensor_tensor(u[:, :], t[:, :], t[:, :], ALU.mult))
                chain.link(nc.vector.scalar_tensor_tensor(out=u[:, :], in0=v[:, :], scalar=4.0 / D, in1=u[:, :],
                                                          op0=ALU.mult, op1=ALU.add))
                chain.link(nc.vector.tensor_scalar(v[:, :], u[:, :], 0.25, EPS, ALU.mult, ALU.add))
                chain.link(nc.vector.tensor_scalar(y[:, :].bitcast(I32), v[:, :].bitcast(I32), -0.5, RSQRT_MAGIC,
                                                   ALU.mult, ALU.add))
                for i in range(3):
                    chain.link(nc.vector.tensor_tensor(t[:, :], y[:, :], y[:, :], ALU.mult))
                    chain.link(nc.vector.scalar_tensor_tensor(out=u[:, :], in0=t[:, :], scalar=-0.5, in1=v[:, :],
                                                              op0=ALU.mult, op1=ALU.mult))
                    dst = y if i < 2 else ln["rstd"][s.par]
                    chain.link(nc.vector.scalar_tensor_tensor(out=dst[:, :], in0=u[:, :], scalar=1.5, in1=y[:, :],
                                                              op0=ALU.add, op1=ALU.mult))
                nc.vector.scalar_tensor_tensor(out=ln["shift"][s.par][:, :], in0=mean2[:, :], scalar=-0.5,
                                               in1=ln["rstd"][s.par][:, :], op0=ALU.mult, op1=ALU.mult).then_inc(done, 1)
                chain.end()

            def stats_chain(s_):
                return Chain(dve, s_, LN_PER - 1)

            def route_stats(layer, s):
                wait(dve, rn_done[layer], BATCH * (s.n - 1))
                layer_norm_stats(ln_route, stats_chain(ln_chain[layer]), s,
                                 lambda b: res[:, bass.ds(s.n * BATCH * D + b * D, D)], ln_done[layer])

            def route_logits(layer, s):
                dve.wait_ge(logits_ready[layer], s.n + 1)
                n = BATCH * EXPERTS
                nc.vector.tensor_tensor(
                    logits[:, bass.ds(s.n * n, n)].rearrange("p (b e) -> p b e", e=EXPERTS),
                    bank[4][:, 0:n].rearrange("p (b e) -> p b e", e=EXPERTS),
                    br_sb[:, :].unsqueeze(1).to_broadcast([P, BATCH, EXPERTS]), ALU.add).then_inc(logits_added[layer], 1)

            def route(layer):
                chain = Chain(dve, route_chain[layer], 12)
                chain.begin(0)
                dve.wait_ge(logits_added[layer], STEPS)
                by_tile = lambda t: t[:, :].rearrange("p (i e) -> p i e", e=EXPERTS)
                as_tile = lambda t: t[:, :].rearrange("p (e i) -> p i e", e=EXPERTS)
                by_expert = lambda t: t[:, :].rearrange("p (e i) -> p e i", e=EXPERTS)
                spread = lambda t: t[:, :].unsqueeze(2).to_broadcast([P, TOKEN_TILES, EXPERTS])
                chain.link(nc.vector.tensor_reduce(best[:, :], by_tile(logits), AX_X, ALU.max))
                chain.link(nc.vector.tensor_tensor(by_tile(pick), by_tile(logits), spread(best), ALU.is_equal))
                chain.link(nc.vector.tensor_tensor(by_tile(pick), by_tile(pick),
                                                   cst("prefer").unsqueeze(1).to_broadcast([P, TOKEN_TILES, EXPERTS]), ALU.mult))
                chain.link(nc.vector.tensor_reduce(best[:, :], by_tile(pick), AX_X, ALU.max))
                chain.link(nc.vector.tensor_tensor(as_tile(onehot), by_tile(pick), spread(best), ALU.is_equal))
                nc.vector.tensor_copy(onehot_bf[:, :], onehot[:, :]).then_inc(onehot_ready[layer], 1)
                dve.wait_ge(counts_ready[layer], 1)
                n = TOKEN_TILES * EXPERTS
                chain.link(nc.vector.tensor_copy(total[:, :], bank[6][:, 0:n]))
                chain.link(nc.vector.tensor_tensor_scan(upto[:, :], cst("not_first"), total[:, :], 0.0, ALU.mult, ALU.add))
                nc.vector.tensor_scalar(tiles_e[:, :], by_expert(upto)[:, :, TOKEN_TILES - 1], P / 2 - 0.5, 1.0 / P,
                                        ALU.add, ALU.mult).then_inc(route_chain[layer], 1)
                chain.k += 1
                nc.vector.tensor_tensor(place[:, :], bank[5][:, 0:n], upto[:, :], ALU.add)
                dve.wait_ge(route_chain[layer], chain.k)
                chain.link(nc.vector.tensor_scalar(tiles_e[:, :], tiles_e[:, :], ROUND, -ROUND, ALU.add, ALU.add))
                chain.link(nc.vector.tensor_tensor_scan(ends_e[:, :], cst("ones")[:, 0:EXPERTS], tiles_e[:, :], 0.0,
                                                        ALU.mult, ALU.add))
                chain.link(nc.vector.tensor_tensor(base_e[:, :], ends_e[:, :], tiles_e[:, :], ALU.subtract))
                place_chain = [0]

                def link(ins):
                    place_chain[0] += 1
                    ins.then_inc(slots_chain[layer], 1)
                    dve.wait_ge(slots_chain[layer], place_chain[0])

                link(nc.vector.tensor_tensor(place[:, :], place[:, :], total[:, :], ALU.subtract))
                link(nc.vector.scalar_tensor_tensor(out=by_expert(place), in0=base_e[:, :].unsqueeze(2).to_broadcast(
                    [P, EXPERTS, TOKEN_TILES]), scalar=float(P), in1=by_expert(place), op0=ALU.mult, op1=ALU.add))
                link(nc.vector.tensor_tensor(place[:, :], place[:, :], onehot[:, :], ALU.mult))
                nc.vector.tensor_reduce(slot_of_f[:, :], as_tile(place), AX_X, ALU.add).then_inc(slots_chain[layer], 1)
                dve.wait_ge(slots_chain[layer], place_chain[0] + 1)
                nc.vector.tensor_copy(slot_of[layer][:, :], slot_of_f[:, :]).then_inc(slots_known[layer], 1)
                link2 = place_chain[0] + 1
                nc.vector.tensor_tensor(ended[:, :].rearrange("p (j e) -> p j e", e=EXPERTS),
                                        ends_e[0:1, :].unsqueeze(1).to_broadcast([1, SLOT_TILES, EXPERTS]),
                                        cst("slot_tile", 1).unsqueeze(2).to_broadcast([1, SLOT_TILES, EXPERTS]),
                                        ALU.is_le).then_inc(slots_chain[layer], 1)
                dve.wait_ge(slots_chain[layer], link2 + 1)
                nc.vector.tensor_reduce(owner_f[:, :], ended[:, :].rearrange("p (j e) -> p j e", e=EXPERTS),
                                        AX_X, ALU.add).then_inc(slots_chain[layer], 1)
                dve.wait_ge(slots_chain[layer], link2 + 2)
                nc.vector.tensor_scalar(owner[layer][:, :], owner_f[:, :], float(EXPERTS - 1), None,
                                        ALU.min).then_inc(owners_known[layer], 1)

            def expert_layer(layer):
                def add_b1(t, par):
                    dve.wait_ge(up_done[layer], t + 1)
                    wait(dve, hT_ready[layer], t - 1)
                    e = dve.value_load(owner[layer][0:1, bass.ds(t, 1)], min_val=0, max_val=EXPERTS - 1)
                    nc.vector.tensor_tensor(h_pre[par][:, :], bank[2 + par][:, :], b1_sb[:, bass.ds(e * FF, FF)],
                                            ALU.add).then_inc(b1_added[layer], 1)

                def add_b2(t, par):
                    dve.wait_ge(down_done[layer], t + 1)
                    e = dve.value_load(owner[layer][0:1, bass.ds(t, 1)], min_val=0, max_val=EXPERTS - 1)
                    nc.vector.tensor_tensor(slot_y[:, bass.ds(t * D, D)], bank[6 + par][:, 0:D],
                                            b2_sb[:, bass.ds(e * D, D)], ALU.add).then_inc(b2_added[layer], 1)

                dve.wait_ge(owners_known[layer], 1)
                if layer == 0:
                    dve.wait_ge(slots_cleared, 16)
                else:
                    dve.wait_ge(y_stored[0], 16 * SLOT_TILES)
                def sums(k, it=0):
                    if k < SLOT_TILES:
                        add_b1(2 * it + k, k % 2)
                    if k >= 2:
                        add_b2(2 * it + k - 2, k % 2)

                rolled(dve, sums, 0, 4, SLOT_TILES, SLOT_TILES + 2)

            def mix_in(s):
                dve.wait_ge(fetched[0][s.par], 16 * BATCH * (s.half + 1))
                nc.vector.scalar_tensor_tensor(out=of_step(res, s), in0=back[s.par][:, :], scalar=0.5, in1=of_step(res, s),
                                               op0=ALU.mult, op1=ALU.add).then_inc(mixed_in, 1)
                dve.wait_ge(mixed_in, s.n + 1)
                wait(dve, xn_done, BATCH * (s.n - 1))
                layer_norm_stats(ln_attn, stats_chain(la_chain), s,
                                 lambda b: res[:, bass.ds(s.n * BATCH * D + b * D, D)], la_done)

            def front(s):
                dve.wait_ge(qkv_done, BATCH * (s.n + 1))
                wait(dve, delta_ready, s.n - 1)
                k_ = qkv[s.par][:, :].rearrange("p (b w) -> p b w", b=BATCH)[:, :, D:2 * D]
                nc.vector.tensor_tensor(per_batch(kd[s.par][:, :]), k_,
                                        cst("decay_k").unsqueeze(1).to_broadcast([P, BATCH, D]),
                                        ALU.mult).then_inc(kd_done, 1)
                dve.wait_ge(qT_ready, s.n + 1)
                wait(dve, inter_ready, s.n - 1)
                nc.vector.tensor_tensor(per_batch(qdT[s.par][:, :]), per_batch(bank[5][:, :]),
                                        cst("decay_q").unsqueeze(1).to_broadcast([P, BATCH, P]),
                                        ALU.mult).then_inc(qdT_done, 1)

            def states(s):
                q_ = qkv[s.par][:, :].rearrange("p (b w) -> p b w", b=BATCH)

                def times_q(h):
                    wait(dve, o_in_done, PAIRS * s.n + h - 1)
                    dve.wait_ge(state_ready, PAIRS * s.n + h + 1)
                    q2 = q_[:, :, h * 2 * HD:(h + 1) * 2 * HD].unsqueeze(3).to_broadcast([P, BATCH, 2 * HD, HD])
                    nc.vector.tensor_tensor(qS[h % 2][:, :].rearrange("p (b a e) -> p b a e", b=BATCH, e=HD),
                                            bank[h % 3][:, :].rearrange("p (b a e) -> p b a e", b=BATCH, e=HD),
                                            q2, ALU.mult).then_inc(qS_done, 1)

                def sum_d(h):
                    dve.wait_ge(qS_done, PAIRS * s.n + h + 1)
                    w = BATCH * 2 * HD
                    nc.vector.tensor_reduce(o_in[:, h * w:(h + 1) * w].rearrange("p (a e) -> p a e", e=HD),
                                            qS[h % 2][:, :].rearrange("p (a d e) -> p a e d", d=HD, e=HD),
                                            AX_X, ALU.add).then_inc(o_in_done, 1)

                times_q(0)
                for h in range(PAIRS):
                    if h + 1 < PAIRS:
                        times_q(h + 1)
                    sum_d(h)

            def join(s):
                dve.wait_ge(inter_ready, s.n + 1)
                dve.wait_ge(o_in_done, PAIRS * (s.n + 1))
                wait(dve, on_done, BATCH * s.n)
                w2 = 2 * HD
                nc.vector.tensor_tensor(
                    o_all[:, :].rearrange("p (b h w) -> p b h w", b=BATCH, w=w2),
                    bank[7][:, :].rearrange("p (b h w) -> p b h w", b=BATCH, w=w2),
                    o_in[:, :].rearrange("p (h b w) -> p b h w", b=BATCH, w=w2), ALU.add).then_inc(o_done, 1)
                dve.wait_ge(o_done, s.n + 1)
                layer_norm_stats(ln_out, stats_chain(lo_chain), s, lambda b: o_all[:, b * D:(b + 1) * D], lo_done)

            def update_carry(s):
                dve.wait_ge(delta_ready, s.n + 1)
                nc.vector.tensor_tensor(per_batch(carry_new[:, :]), per_batch(bank[6][:, :]),
                                        cst("carry_mask").unsqueeze(1).to_broadcast([P, BATCH, D]),
                                        ALU.mult).then_inc(delta_masked, 1)
                dve.wait_ge(delta_masked, s.n + 1)
                nc.vector.scalar_tensor_tensor(out=carry[:, :], in0=carry[:, :], scalar=cst("decay_c"), in1=carry_new[:, :],
                                               op0=ALU.mult, op1=ALU.add).then_inc(carry_done, 1)

            def gate(s):
                dve.wait_ge(onT_copied, s.n + 1)
                dve.wait_ge(gate_done, s.n + 1)
                wait(dve, wo_ready, s.n)
                nc.vector.scalar_tensor_tensor(out=o_gT[:, :], in0=gateT[s.par][:, :], scalar=1.0, in1=o_nT[:, :],
                                               op0=ALU.add, op1=ALU.mult).then_inc(gated, 1)

            def residual(s):
                dve.wait_ge(wo_ready, s.n + 1)
                nc.vector.scalar_tensor_tensor(out=of_step(res, s), in0=bank[7][:, :], scalar=0.5, in1=of_step(res, s),
                                               op0=ALU.mult, op1=ALU.add).then_inc(res_done, 1)

            def attention(k, it=0):
                cur = step(k, it) if 0 <= k < STEPS else None
                nxt = step(k + 1, it) if k + 1 < STEPS else None
                prv = step(k - 1, it) if k >= 1 else None
                if nxt is not None:
                    mix_in(nxt)
                if cur is not None:
                    states(cur)
                    join(cur)
                if nxt is not None:
                    front(nxt)
                if cur is not None:
                    update_carry(cur)
                if prv is not None:
                    dve.wait_ge(res_done, prv.n + 1)
                    route_stats(1, prv)
                if cur is not None:
                    gate(cur)
                    residual(cur)
                if prv is not None:
                    route_logits(1, prv)

            dve.wait_ge(const_loaded, 16)
            nc.vector.tensor_copy(upper_bf[:, :], cst("upper"))
            nc.vector.tensor_copy(ones_bf[:, :], cst("ones")).then_inc(bf_ready, 1)
            nc.vector.memset(carry[:, :], 0.0).then_inc(carry_done, 1)
            dve.wait_ge(carry_done, 1)
            dve.wait_ge(router_loaded, 32)
            dve.wait_ge(x_loaded[0], 16 * BATCH)
            dve.wait_ge(x_loaded[1], 16 * BATCH)
            def route_step(k, it=0):
                if k < STEPS:
                    route_stats(0, step(k, it))
                if k >= 1:
                    route_logits(0, step(k - 1, it))

            rolled(dve, route_step, 0, 3, STEPS - 1, STEPS + 1)
            route(0)
            dve.wait_ge(expert_w_loaded, 64)
            expert_layer(0)
            rolled(dve, attention, -1, 2, STEPS - 1, STEPS + 1)
            route(1)
            expert_layer(1)

            def finish(s):
                dve.wait_ge(fetched[1][s.par], 16 * BATCH * (s.half + 1))
                nc.vector.scalar_tensor_tensor(out=of_step(res, s), in0=back[s.par][:, :], scalar=0.5, in1=of_step(res, s),
                                               op0=ALU.mult, op1=ALU.add).then_inc(final_done, 1)

            with dve.Fori(0, STEPS // 2) as it:
                for k in range(2):
                    finish(step(k, it))

        @block.tensor
        def _(pe):
            mm = nc.tensor.matmul

            def transpose4(dst, src, done):
                for b in range(BATCH):
                    last = nc.tensor.transpose(dst[:, b * P:(b + 1) * P], src(b), ident)
                last.then_inc(done, 1)

            def route_transpose(layer, s):
                pe.wait_ge(rn_done[layer], BATCH * (s.n + 1))
                wait(pe, rnT_copied[layer], s.n)
                if layer == 1:
                    wait(pe, qkv_done, 1)
                transpose4(bank[3], lambda b: rn[s.par][:, b * D:(b + 1) * D], rnT_ready[layer])

            def route_product(layer, s):
                pe.wait_ge(rnT_copied[layer], s.n + 1)
                wait(pe, logits_added[layer], s.n)
                for b in range(BATCH):
                    last = mm(bank[4][:, b * EXPERTS:(b + 1) * EXPERTS], rnT[s.par][:, b * P:(b + 1) * P], wr_sb[:, :],
                              start=True, stop=True)
                last.then_inc(logits_ready[layer], 1)

            def route_counts(layer):
                pe.wait_ge(onehot_ready[layer], 1)
                n = TOKEN_TILES * EXPERTS
                mm(bank[5][:, 0:n], upper_bf[:, :], onehot_bf[:, :], start=True, stop=True)
                mm(bank[6][:, 0:n], ones_bf[:, :], onehot_bf[:, :], start=True, stop=True).then_inc(counts_ready[layer], 1)

            def expert_layer(layer):
                def load_expert(t):
                    return pe.value_load(owner[layer][0:1, bass.ds(t, 1)], min_val=0, max_val=EXPERTS - 1)

                def slot_transpose(s):
                    pe.wait_ge(slot_loaded[layer][s.par], 16 * (s.half + 1))
                    wait(pe, slotT_copied[layer], s.n - 1)
                    nc.tensor.transpose(bank[s.par][:, 0:P], slot_x[s.par][:, :], ident).then_inc(slotT_ready[layer], 1)

                def up(s):
                    pe.wait_ge(slotT_copied[layer], s.n + 1)
                    wait(pe, b1_added[layer], s.n - 1)
                    e = load_expert(s.n)
                    mm(bank[2 + s.par][:, :], slotT[s.par][:, :], w1_sb[:, bass.ds(e * FF, FF)],
                       start=True, stop=True).then_inc(up_done[layer], 1)

                def h_transpose(s):
                    pe.wait_ge(b1_added[layer], s.n + 1)
                    wait(pe, hT_copied[layer], s.n - 1)
                    for f in range(FB):
                        last = nc.tensor.transpose(bank[4 + s.par][:, f * P:(f + 1) * P],
                                                   h_pre[s.par][:, f * P:(f + 1) * P], ident)
                    last.then_inc(hT_ready[layer], 1)

                def down(s):
                    pe.wait_ge(hT_copied[layer], s.n + 1)
                    wait(pe, b2_added[layer], s.n - 1)
                    e = load_expert(s.n)
                    for f in range(FB):
                        last = mm(bank[6 + s.par][:, 0:D], h_T[s.par][:, f * P:(f + 1) * P],
                                  w2_sb[:, bass.ds(e * FF + f * D, D)], start=(f == 0), stop=(f == FB - 1))
                    last.then_inc(down_done[layer], 1)

                def stages(k, it=0):
                    if k + 1 < SLOT_TILES:
                        slot_transpose(step(k + 1, it))
                    if 0 <= k < SLOT_TILES:
                        up(step(k, it))
                    if 0 <= k - 1 < SLOT_TILES:
                        h_transpose(step(k - 1, it))
                    if 0 <= k - 2:
                        down(step(k - 2, it))

                pe.wait_ge(owners_known[layer], 1)
                rolled(pe, stages, -1, 4, SLOT_TILES - 1, SLOT_TILES + 2)

            def norm_transpose(s):
                pe.wait_ge(xn_done, BATCH * (s.n + 1))
                wait(pe, onT_copied, s.n - 1)
                transpose4(bank[5], lambda b: xn[s.par][:, b * D:(b + 1) * D], xnT_ready)

            def project(s, b):
                pe.wait_ge(xnT_copied, s.n + 1)
                wait(pe, qkv_done, BATCH * s.n + b - 1)
                if b == 0:
                    wait(pe, rnT_copied[1], s.n - 2)
                if b == 1:
                    wait(pe, logits_added[1], s.n - 2)
                mm(bank[3 + b % 2][:, 0:3 * D], xnT[s.par][:, b * P:(b + 1) * P], wqkv_sb[:, :],
                   start=True, stop=True).then_inc(qkv_ready, 1)

            def gate_product(s):
                wait(pe, delta_masked, s.n - 1)
                mm(bank[6][:, :], wg_sb[:, :], xnT[s.par][:, :], start=True, stop=True).then_inc(gate_ready, 1)

            def state_product(s, h):
                pe.wait_ge(outer_done, s.n + 1)
                before = PAIRS * s.n + h - 3 if h >= 3 else PAIRS * (s.n - 1) + 6 + h if h < 2 else PAIRS * (s.n - 1) + 5
                wait(pe, qS_done, before + 1)
                for a in range(2):
                    u = outer[s.par][:, :].rearrange("p (b w) -> p b w", b=BATCH)[:, :, (2 * h + a) * UH:(2 * h + a + 1) * UH]
                    to = bank[h % 3][:, :].rearrange("p (b a w) -> p b a w", b=BATCH, a=2)[:, :, a, :]
                    last = mm(to, decay_sb[:, (2 * h + a) * P:(2 * h + a + 1) * P], u, start=True, stop=True)
                last.then_inc(state_ready, 1)

            def inter_product(s):
                pe.wait_ge(qdT_done, s.n + 1)
                pe.wait_ge(carry_done, s.n + 1)
                wait(pe, res_done, s.n)
                for b in range(BATCH):
                    last = mm(bank[7][:, b * D:(b + 1) * D], qdT[s.par][:, b * P:(b + 1) * P], carry[:, b * D:(b + 1) * D],
                              start=True, stop=True)
                last.then_inc(inter_ready, 1)

            def carry_product(s, has_next):
                pe.wait_ge(kd_done, s.n + 1)
                pe.wait_ge(gate_done, s.n + 1 + has_next)
                for b in range(BATCH):
                    v_ = qkv[s.par][:, b * 3 * D + 2 * D:(b + 1) * 3 * D]
                    last = mm(bank[6][:, b * D:(b + 1) * D], kd[s.par][:, b * D:(b + 1) * D], v_, start=True, stop=True)
                last.then_inc(delta_ready, 1)

            def q_transpose(s):
                pe.wait_ge(qkv_done, BATCH * (s.n + 1))
                transpose4(bank[5], lambda b: qkv[s.par][:, b * 3 * D:b * 3 * D + D], qT_ready)

            def out_transpose(s, has_next):
                pe.wait_ge(on_done, BATCH * (s.n + 1))
                pe.wait_ge(qdT_done, s.n + 1 + has_next)
                transpose4(bank[5], lambda b: o_n[:, b * D:(b + 1) * D], onT_ready)

            def out_product(s):
                pe.wait_ge(gated, s.n + 1)
                pe.wait_ge(o_done, s.n + 1)
                for b in range(BATCH):
                    last = mm(bank[7][:, b * D:(b + 1) * D], o_gT[:, b * P:(b + 1) * P], wo_sb[:, :], start=True, stop=True)
                last.then_inc(wo_ready, 1)

            def attention(k, it=0):
                cur = step(k, it) if 0 <= k < STEPS else None
                nxt = step(k + 1, it) if k + 1 < STEPS else None
                prv = step(k - 1, it) if k >= 1 else None
                for h in range(PAIRS):
                    if cur is not None:
                        state_product(cur, h)
                    if nxt is not None:
                        if h == 2:
                            norm_transpose(nxt)
                        if 3 <= h < 3 + BATCH:
                            project(nxt, h - 3)
                if nxt is not None:
                    gate_product(nxt)
                if cur is not None:
                    inter_product(cur)
                    carry_product(cur, int(nxt is not None))
                if nxt is not None:
                    q_transpose(nxt)
                if cur is not None:
                    out_transpose(cur, int(nxt is not None))
                if prv is not None:
                    route_transpose(1, prv)
                if cur is not None:
                    out_product(cur)
                if prv is not None:
                    route_product(1, prv)

            pe.wait_ge(const_loaded, 16)
            pe.wait_ge(router_loaded, 32)
            def route_step(k, it=0):
                if k < STEPS:
                    route_transpose(0, step(k, it))
                if k >= 1:
                    route_product(0, step(k - 1, it))

            rolled(pe, route_step, 0, 3, STEPS - 1, STEPS + 1)
            pe.wait_ge(attn_w_loaded, 16 * 6)
            mm(bank[7][:, 0:D], wg1_sb[:, :], wg2_sb[:, :], start=True, stop=True).then_inc(wg_ready, 1)
            pe.wait_ge(bf_ready, 1)
            route_counts(0)
            pe.wait_ge(expert_w_loaded, 64)
            pe.wait_ge(wg_copied, 1)
            expert_layer(0)
            pe.wait_ge(decay_loaded, 16)
            rolled(pe, attention, -1, 2, STEPS - 1, STEPS + 1)
            route_counts(1)
            expert_layer(1)


def head_slopes():
    start = 2.0 ** (-2.0 ** (-(np.log2(HEADS) - 3)))
    s = np.array([start * start ** i for i in range(HEADS)], dtype=np.float32)
    return (s * np.float32(1.0 + 1e-05)).astype(np.float64)


def constants():
    s, i = head_slopes(), np.arange(P, dtype=np.float64)
    diff = i[None, :] - i[:, None]
    decay = np.where(diff >= 0, np.exp(-s[:, None, None] * np.maximum(diff, 0)), 0.0)
    per_row = np.repeat(s, HD)
    head = np.arange(P) // HD
    parts = {
        "ident": np.eye(P),
        "carry_mask": head[:, None] == head[None, :],
        "decay_q": np.exp(-per_row[:, None] * (i[None, :] + 1)),
        "decay_k": np.exp(-per_row[None, :] * (P - 1 - i[:, None])),
        "decay_c": np.exp(-per_row[:, None] * P),
        "upper": diff > 0,
        "ones": np.ones((P, P)),
        "not_first": np.tile((np.arange(EXPERTS * TOKEN_TILES) % TOKEN_TILES != 0)[None, :], (P, 1)),
        "prefer": np.tile((EXPERTS - np.arange(EXPERTS))[None, :], (P, 1)),
        "slot_tile": np.tile(np.arange(SLOT_TILES)[None, :], (P, 1)),
    }
    const = np.concatenate([np.asarray(parts[n], dtype=np.float64) for n in CONST], axis=1).astype(np.float32)
    return decay.transpose(1, 0, 2).reshape(P, HEADS * P).astype(np.float32), const


def kernel(**inputs):
    import concourse.bacc as bacc
    from concourse.bass_utils import run_bass_kernel_spmd

    a = {k: np.asarray(v) for k, v in inputs.items()}
    decay, const = constants()
    w2 = a["L0_ffn_W2"].reshape(EXPERTS, D, FB, P)
    arrays = {
        "x": a["L0_attn_x"].reshape(BATCH * SEQ, D),
        "w1t": a["L0_ffn_W1"].transpose(2, 0, 1).reshape(D, EXPERTS * FF),
        "b1": a["L0_ffn_b1"].reshape(EXPERTS * FF),
        "w2t": w2.transpose(3, 0, 2, 1).reshape(P, EXPERTS * FB * D),
        "b2": a["L0_ffn_b2"].reshape(EXPERTS * D),
        "wrt": a["L0_ffn_Wr"].T,
        "br": a["L0_ffn_br"],
        "wqkv": np.concatenate([a["L0_attn_Wq"], a["L0_attn_Wk"], a["L0_attn_Wv"]], axis=1),
        "wg1t": a["L0_attn_Wg1"].T,
        "wg2": a["L0_attn_Wg2"],
        "wo": a["L0_attn_Wo"],
        "gamma": a["L0_attn_gamma"].reshape(D, 1),
        "beta": a["L0_attn_beta"].reshape(D, 1),
        "decay": decay,
        "const": const,
    }
    nc = bacc.Bacc("TRN2", target_bir_lowering=False, num_devices=1)
    arrays = {f"in_{k}": np.ascontiguousarray(v) for k, v in arrays.items()}
    args = [nc.dram_tensor(k, v.shape, mybir.dt.from_np(v.dtype), kind="ExternalInput").ap() for k, v in arrays.items()]
    out = nc.dram_tensor("out_x", (BATCH * SEQ, D), F32, kind="ExternalOutput").ap()
    build(nc, *args, out)
    r = run_bass_kernel_spmd(nc, [arrays], core_ids=[0])
    return r.results[0]["out_x"].reshape(BATCH, SEQ, D)
```

```python
from collections import namedtuple
from contextlib import ExitStack

import numpy as np

import concourse.bass as bass
from concourse import mybir

F32 = mybir.dt.float32
BF16 = mybir.dt.bfloat16
I32 = mybir.dt.int32
ALU = mybir.AluOpType
ACT = mybir.ActivationFunctionType
AX_X = mybir.AxisListType.X

P = 128
BATCH, SEQ, D = 4, 1024, 128
STEPS = SEQ // P
TOKEN_TILES = BATCH * STEPS
EXPERTS, FF = 8, 512
FB = FF // P
GROUPS = 2
GROUP_STEPS = STEPS // GROUPS
GROUP_TILES = TOKEN_TILES // GROUPS
SLOT_TILES = GROUP_TILES + EXPERTS - 1
UNITS = 2 * GROUPS
HEADS = 16
HD = D // HEADS
PAIRS = HEADS // 2
UH = HD * HD
UW = HEADS * UH
EPS = 1e-5
ROUND = 1.5 * 2.0 ** 23
RSQRT_MAGIC = float(0x5F3759DF)

CONST = {}
_at = 0
for _name, _width in (("ident", P), ("carry_mask", P), ("decay_q", P), ("decay_k", P), ("decay_c", 1),
                      ("upper", P), ("ones", P), ("not_first", EXPERTS * GROUP_TILES),
                      ("prefer", EXPERTS), ("slot_tile", SLOT_TILES)):
    CONST[_name] = (_at, _width)
    _at += _width
CONST_W = _at

Step = namedtuple("Step", "n half par")


def step(k, it=0):
    return Step(2 * it + k, it + k // 2, k % 2)


def wait(eng, sem, value):
    if isinstance(value, int) and value <= 0:
        return
    eng.wait_ge(sem, value)


def rolled(eng, body, first, loop_from, loop_to, end):
    for k in range(first, loop_from):
        body(k)
    with eng.Fori(0, (loop_to - loop_from) // 2) as it:
        for k in (loop_from, loop_from + 1):
            body(k, it)
    for k in range(loop_from + (loop_to - loop_from) // 2 * 2, end):
        body(k)


class Chain:

    def __init__(self, eng, sem):
        self.eng, self.sem, self.k = eng, sem, 0

    def link(self, ins):
        self.k += 1
        ins.then_inc(self.sem, 1)
        self.eng.wait_ge(self.sem, self.k)


def build(nc, x, w1t, b1, w2t, b2, wrt, br, wqkv, wg1t, wg2, wo, gamma, beta, decay, const, out):
    with ExitStack() as ctx:
        def sb(name, shape, dt=F32):
            return ctx.enter_context(nc.sbuf_tensor(name, shape, dt))

        def pb(name, shape=(P, 512)):
            return ctx.enter_context(nc.psum_tensor(name, list(shape), F32))

        def sem(name):
            return ctx.enter_context(nc.semaphore(name))

        slots_in = [nc.dram_tensor(f"slots_in{g}", (SLOT_TILES * P, D), F32, kind="Internal").ap() for g in range(GROUPS)]
        slots_out = [nc.dram_tensor(f"slots_out{g}", (SLOT_TILES * P, D), F32, kind="Internal").ap() for g in range(GROUPS)]

        res = sb("res", [P, TOKEN_TILES * D])
        normed = sb("normed", [P, TOKEN_TILES * D])
        w1_sb = sb("w1_sb", [P, EXPERTS * FF])
        w2_sb = sb("w2_sb", [P, EXPERTS * FF])
        b1_sb = sb("b1_sb", [P, EXPERTS * FF])
        b2_sb = sb("b2_sb", [P, EXPERTS * D])
        decay_sb = sb("decay_sb", [P, HEADS * P])
        const_sb = sb("const_sb", [P, CONST_W])
        wr_sb = sb("wr_sb", [P, EXPERTS])
        br_sb = sb("br_sb", [P, EXPERTS])
        wqkv_sb = sb("wqkv_sb", [P, 3 * D])
        wo_sb = sb("wo_sb", [P, D])
        wg1_sb = sb("wg1_sb", [HD, D])
        wg2_sb = sb("wg2_sb", [HD, D])
        wg_sb = sb("wg_sb", [P, D])
        gb_sb = sb("gb_sb", [P, 2])
        upper_bf = sb("upper_bf", [P, P], BF16)
        ones_bf = sb("ones_bf", [P, P], BF16)

        xn = [sb(f"xn{i}", [P, BATCH * D]) for i in range(2)]
        xnT = [sb(f"xnT{i}", [P, BATCH * P]) for i in range(2)]
        rn = [sb(f"rn{i}", [P, BATCH * D]) for i in range(2)]
        rnT = [sb(f"rnT{i}", [P, BATCH * P]) for i in range(2)]
        qkv = [sb(f"qkv{i}", [P, BATCH * 3 * D]) for i in range(2)]
        gateT = [sb(f"gateT{i}", [P, BATCH * P]) for i in range(2)]
        outer = [sb(f"outer{i}", [P, BATCH * UW]) for i in range(2)]
        zeros = outer[0][:, 0:SLOT_TILES * D]
        slot_y = outer[1][:, 0:SLOT_TILES * D]
        kd = [sb(f"kd{i}", [P, BATCH * D]) for i in range(2)]
        qdT = [sb(f"qdT{i}", [P, BATCH * P]) for i in range(2)]
        qS = [sb(f"qS{i}", [P, 512]) for i in range(3)]
        o_in = sb("o_in", [P, BATCH * D])
        o_all = sb("o_all", [P, BATCH * D])
        o_n = sb("o_n", [P, BATCH * D])
        o_nT = sb("o_nT", [P, BATCH * P])
        o_gT = sb("o_gT", [P, BATCH * P])
        carry = sb("carry", [P, BATCH * D])
        carry_new = sb("carry_new", [P, BATCH * D])
        h_pre, h_T = kd, qdT
        slot_x = [o_all[:, i * D:(i + 1) * D] for i in range(2)]
        slotT = [o_all[:, (2 + i) * D:(3 + i) * D] for i in range(2)]

        logits = sb("logits", [P, TOKEN_TILES * EXPERTS])
        onehot = sb("onehot", [P, GROUP_TILES * EXPERTS])
        onehot_bf = sb("onehot_bf", [P, GROUP_TILES * EXPERTS], BF16)
        total = sb("total", [P, GROUP_TILES * EXPERTS])
        upto = sb("upto", [P, GROUP_TILES * EXPERTS])
        place = sb("place", [P, GROUP_TILES * EXPERTS])
        pick = place
        best = sb("best", [P, GROUP_TILES])
        tiles_e = sb("tiles_e", [P, EXPERTS])
        ends_e = sb("ends_e", [P, EXPERTS])
        base_e = sb("base_e", [P, EXPERTS])
        ended = sb("ended", [1, SLOT_TILES * EXPERTS])
        slot_of_f = sb("slot_of_f", [P, GROUP_TILES])
        owner_f = sb("owner_f", [1, SLOT_TILES])
        owner = [sb(f"owner{u}", [1, SLOT_TILES], I32) for u in range(UNITS)]
        slot_of = [sb(f"slot_of{u}", [P, GROUP_TILES], I32) for u in range(UNITS)]

        AHEAD, OUTPUT, ROUTED = 0, BATCH, 2 * BATCH
        LN_W = max(3 * BATCH, GROUP_TILES)
        st = sb("st", [P, LN_W, 6])
        mean2, var, yy, tt, uu = (sb(n, [P, LN_W]) for n in ("mean2", "var", "yy", "tt", "uu"))
        rstd = [sb(f"rstd{i}", [P, LN_W]) for i in range(2)]
        shift = [sb(f"shift{i}", [P, LN_W]) for i in range(2)]

        bank = [pb(f"bank{i}") for i in range(8)]

        def cst(name, rows=P):
            a, w = CONST[name]
            return const_sb[0:rows, a:a + w]

        ident = cst("ident")
        per_batch = lambda ap, w=D: ap.rearrange("p (b d) -> p b d", b=BATCH)
        of_step = lambda t, s, w=BATCH * D: t[:, bass.ds(s.n * w, w)]

        x_loaded = [sem(f"x_loaded{i}") for i in range(2)]
        const_loaded, decay_loaded = sem("const_loaded"), sem("decay_loaded")
        router_loaded, attn_w_loaded, expert_w_loaded = sem("router_loaded"), sem("attn_w_loaded"), sem("expert_w_loaded")
        zeroed, slots_cleared = sem("zeroed"), sem("slots_cleared")
        bf_ready, wg_ready, wg_copied = sem("bf_ready"), sem("wg_ready"), sem("wg_copied")
        by_unit = lambda name: [sem(f"{name}{u}") for u in range(UNITS)]
        rn_done, rnT_ready, rnT_copied, rows_kept = sem("rn_done"), sem("rnT_ready"), sem("rnT_copied"), sem("rows_kept")
        logits_ready, logits_added = sem("logits_ready"), sem("logits_added")
        ln_chain0 = [sem(f"ln_chain0_{g}") for g in range(GROUPS)]
        route_chain, onehot_ready, counts_ready, slots_known, owners_known = (
            by_unit("route_chain"), by_unit("onehot_ready"), by_unit("counts_ready"), by_unit("slots_known"),
            by_unit("owners_known"))
        slots_chain = by_unit("slots_chain")
        rows_sorted, fetched = by_unit("rows_sorted"), by_unit("fetched")
        slot_loaded = [[sem(f"slot_loaded{u}_{p}") for p in range(2)] for u in range(UNITS)]
        slotT_ready, slotT_copied, up_done, b1_added, hT_ready, hT_copied, down_done, b2_added, y_stored = (
            by_unit("slotT_ready"), by_unit("slotT_copied"), by_unit("up_done"), by_unit("b1_added"), by_unit("hT_ready"),
            by_unit("hT_copied"), by_unit("down_done"), by_unit("b2_added"), by_unit("y_stored"))
        ln_chain, ln_ready, xn_done, xnT_ready, xnT_copied = (
            sem("ln_chain"), sem("ln_ready"), sem("xn_done"), sem("xnT_ready"), sem("xnT_copied"))
        qkv_ready, qkv_done, gate_ready, gate_done = sem("qkv_ready"), sem("qkv_done"), sem("gate_ready"), sem("gate_done")
        outer_done, kd_done, qT_ready, qdT_done = sem("outer_done"), sem("kd_done"), sem("qT_ready"), sem("qdT_done")
        state_ready, qS_done, o_in_done = sem("state_ready"), sem("qS_done"), sem("o_in_done")
        inter_ready, o_done, delta_ready, delta_masked, carry_done = (
            sem("inter_ready"), sem("o_done"), sem("delta_ready"), sem("delta_masked"), sem("carry_done"))
        on_done, onT_ready, onT_copied, gated, wo_ready, res_done = (
            sem("on_done"), sem("onT_ready"), sem("onT_copied"), sem("gated"),
            sem("wo_ready"), sem("res_done"))
        b2_halved, out_stored = sem("b2_halved"), sem("out_stored")

        block = ctx.enter_context(nc.Block())

        @block.sync
        def _(sp):
            x_v = x.rearrange("(b c p) d -> p c b d", b=BATCH, p=P)
            res_v = res[:, :].rearrange("p (c b d) -> p c b d", c=STEPS, b=BATCH)
            for g in range(GROUPS):
                c0 = g * GROUP_STEPS
                for b in range(BATCH):
                    sp.dma_start(res_v[:, c0:c0 + GROUP_STEPS, b, :], x_v[:, c0:c0 + GROUP_STEPS, b, :]).then_inc(x_loaded[g], 16)
                if g == 0:
                    sp.wait_ge(zeroed, 1)
                sp.dma_start(slots_in[g].rearrange("(t p) d -> p t d", p=P),
                             zeros.rearrange("p (t d) -> p t d", d=D)).then_inc(slots_cleared, 16)

            def experts(u):
                g = u % GROUPS

                def load(s):
                    wait(sp, slotT_ready[u], s.n - 1)
                    sp.dma_start(slot_x[s.par], slots_in[g][bass.ds(s.n * P, P), :]).then_inc(slot_loaded[u][s.par], 16)

                def store(t):
                    sp.wait_ge(b2_added[u], t + 1)
                    sp.dma_start(slots_out[g][bass.ds(t * P, P), :], slot_y[:, bass.ds(t * D, D)]).then_inc(y_stored[u], 16)

                sp.wait_ge(rows_sorted[u], 16 * GROUP_TILES)
                if u % GROUPS:
                    sp.wait_ge(slotT_ready[u - 1], SLOT_TILES)
                if u == GROUPS:
                    sp.wait_ge(on_done, BATCH * STEPS)
                ahead = 5
                for t in range(ahead):
                    load(step(t))
                pairs = (SLOT_TILES - ahead) // 2
                with sp.Fori(0, pairs) as it:
                    for k in range(2):
                        load(step(k + ahead, it))
                        store(2 * it + k)
                with sp.Fori(2 * pairs, SLOT_TILES) as t:
                    store(t)

            for u in range(UNITS):
                experts(u)
            out_v = out.rearrange("(b c p) d -> p c b d", b=BATCH, p=P)
            for g in range(GROUPS):
                sp.wait_ge(fetched[GROUPS + g], 16 * GROUP_TILES)
                c0 = g * GROUP_STEPS
                for b in range(BATCH):
                    sp.dma_start(out_v[:, c0:c0 + GROUP_STEPS, b, :], res_v[:, c0:c0 + GROUP_STEPS, b, :]).then_inc(out_stored, 16)
            sp.wait_ge(out_stored, 16 * GROUPS * BATCH)

        @block.gpsimd
        def _(pool):
            pool.memset(zeros, 0.0).then_inc(zeroed, 1)

            def sort_rows(u):
                pool.wait_ge(rows_kept, u * GROUP_STEPS + GROUP_STEPS)
                pool.wait_ge(slots_known[u], 1)
                if u < GROUPS:
                    pool.wait_ge(slots_cleared, 16 * GROUPS)
                g = u % GROUPS
                for t in range(GROUP_TILES):
                    at = (g * GROUP_TILES + t) * D
                    pool.indirect_dma_start(
                        slots_in[g], bass.IndirectOffsetOnAxis(ap=slot_of[u][:, t:t + 1], axis=0),
                        normed[:, at:at + D], None).then_inc(rows_sorted[u], 16)

            def fetch(u, first, end):
                pool.wait_ge(y_stored[u], 16 * SLOT_TILES)
                g = u % GROUPS
                for t in range(first, end):
                    at = (g * GROUP_TILES + t) * D
                    pool.indirect_dma_start(
                        res[:, at:at + D], None, slots_out[g],
                        bass.IndirectOffsetOnAxis(ap=slot_of[u][:, t:t + 1], axis=0),
                        compute_op=ALU.add).then_inc(fetched[u], 16)

            def outer_products(n):
                par = n % 2
                pool.wait_ge(qkv_done, BATCH * (n + 1))
                wait(pool, state_ready, PAIRS * (n - 1))
                for h in range(2):
                    for b in range(BATCH):
                        w = HEADS // 2
                        at = b * 3 * D + h * w * HD
                        k_ = qkv[par][:, at + D:at + D + w * HD].unsqueeze(2).to_broadcast([P, w * HD, HD])
                        v_ = (qkv[par][:, at + 2 * D:at + 2 * D + w * HD].rearrange("p (h e) -> p h e", e=HD)
                              .unsqueeze(2).to_broadcast([P, w, HD, HD]))
                        u_ = outer[par][:, b * UW + h * w * UH:b * UW + (h + 1) * w * UH]
                        last = pool.tensor_tensor(u_.rearrange("p (h d e) -> p h d e", d=HD, e=HD),
                                                  k_.rearrange("p (h d) e -> p h d e", d=HD), v_, ALU.mult)
                    last.then_inc(outer_done, 1)

            sort_rows(0)
            sort_rows(1)
            fetch(0, 0, GROUP_TILES)
            share = GROUP_TILES // 4
            for n in range(STEPS):
                if n < 4:
                    fetch(1, n * share, (n + 1) * share)
                outer_products(n)
            sort_rows(2)
            sort_rows(3)
            fetch(2, 0, GROUP_TILES)
            fetch(3, 0, GROUP_TILES)

        @block.scalar
        def _(act):
            act.dma_start(const_sb[:, :], const).then_inc(const_loaded, 16)
            act.dma_start(wr_sb[:, :], wrt).then_inc(router_loaded, 16)
            act.dma_start(br_sb[:, :], br.partition_broadcast(P)).then_inc(router_loaded, 16)
            act.wait_ge(x_loaded[0], 16 * BATCH)
            act.dma_start(w1_sb[:, :], w1t).then_inc(expert_w_loaded, 16)
            act.dma_start(b1_sb[:, :], b1.partition_broadcast(P)).then_inc(expert_w_loaded, 16)
            act.dma_start(w2_sb[:, :], w2t).then_inc(expert_w_loaded, 16)
            act.dma_start(b2_sb[:, :], b2.partition_broadcast(P)).then_inc(expert_w_loaded, 16)
            for dst, src in ((wqkv_sb, wqkv), (wo_sb, wo), (wg1_sb, wg1t), (wg2_sb, wg2)):
                act.dma_start(dst[:, :], src).then_inc(attn_w_loaded, 16)
            act.dma_start(gb_sb[:, 0:1], gamma).then_inc(attn_w_loaded, 16)
            act.dma_start(gb_sb[:, 1:2], beta).then_inc(attn_w_loaded, 16)
            act.dma_start(decay_sb[:, :], decay).then_inc(decay_loaded, 16)

            def normalise(dst, src, par, col, done):
                for b in range(BATCH):
                    nc.scalar.activation(dst[:, b * D:(b + 1) * D], src(b), ACT.Identity,
                                         bias=shift[par][:, col + b:col + b + 1],
                                         scale=rstd[par][:, col + b:col + b + 1]).then_inc(done, 1)

            res_tile = lambda s: lambda b: res[:, bass.ds(s.n * BATCH * D + b * D, D)]

            def route_copy(r, par, b3=None):
                act.wait_ge(rnT_ready, r + 1)
                wait(act, logits_ready, r - 1)
                nc.scalar.activation(rnT[par][:, :], bank[3][:, :], ACT.Copy).then_inc(rnT_copied, 1)

            def expert_unit(u):
                def slotT_copy(t, par):
                    act.wait_ge(slotT_ready[u], t + 1)
                    wait(act, up_done[u], t - 1)
                    nc.scalar.activation(slotT[par], bank[par][:, 0:P], ACT.Copy).then_inc(slotT_copied[u], 1)

                def relu_copy(t, par):
                    act.wait_ge(hT_ready[u], t + 1)
                    wait(act, down_done[u], t - 1)
                    nc.scalar.activation(h_T[par][:, :], bank[4 + par][:, :], ACT.Relu).then_inc(hT_copied[u], 1)

                def copies(k, it=0):
                    if k < SLOT_TILES:
                        slotT_copy(2 * it + k, k % 2)
                    if k >= 2:
                        relu_copy(2 * it + k - 2, k % 2)

                if u % GROUPS:
                    act.wait_ge(up_done[u - 1], SLOT_TILES)
                    act.wait_ge(down_done[u - 1], SLOT_TILES)
                rolled(act, copies, 0, 4, SLOT_TILES, SLOT_TILES + 2)

            def attn_front(s):
                act.wait_ge(xnT_ready, s.n + 1)
                wait(act, gate_ready, s.n - 1)
                nc.scalar.activation(xnT[s.par][:, :], bank[5][:, :], ACT.Copy).then_inc(xnT_copied, 1)
                wait(act, qS_done, PAIRS * (s.n - 1))
                wait(act, outer_done, 2 * (s.n - 1))
                wait(act, delta_ready, s.n - 1)
                for b in range(BATCH):
                    act.wait_ge(qkv_ready, BATCH * s.n + b + 1)
                    nc.scalar.activation(qkv[s.par][:, b * 3 * D:(b + 1) * 3 * D], bank[3 + b % 2][:, 0:3 * D],
                                         ACT.Silu).then_inc(qkv_done, 1)

            def gate_tanh(s):
                act.wait_ge(gate_ready, s.n + 1)
                wait(act, gated, s.n - 1)
                nc.scalar.activation(gateT[s.par][:, :], bank[6][:, :], ACT.Tanh, scale=0.5).then_inc(gate_done, 1)

            def attention(k, it=0):
                if 0 <= k + 1 < STEPS:
                    attn_front(step(k + 1, it))
                if 0 <= k < STEPS:
                    gate_tanh(step(k, it))
                here = step(k, it)
                act.wait_ge(ln_ready, here.n + 3)
                if 1 <= k <= STEPS:
                    s = step(k - 1, it)
                    wait(act, onT_ready, s.n)
                    normalise(o_n, lambda b: o_all[:, b * D:(b + 1) * D], here.par, OUTPUT, on_done)
                if k + 2 < STEPS:
                    s = step(k + 2, it)
                    wait(act, xnT_ready, s.n - 1)
                    normalise(xn[s.par], res_tile(s), here.par, AHEAD, xn_done)
                if 1 <= k <= STEPS:
                    s = step(k - 1, it)
                    act.wait_ge(onT_ready, s.n + 1)
                    wait(act, gated, s.n)
                    nc.scalar.activation(o_nT[:, :], bank[5][:, :], ACT.Identity, bias=gb_sb[:, 1:2],
                                         scale=gb_sb[:, 0:1]).then_inc(onT_copied, 1)
                if k >= 2:
                    s = step(k - 2, it)
                    wait(act, rnT_ready, STEPS + s.n - 1)
                    normalise(rn[s.par], res_tile(s), here.par, ROUTED, rn_done)
                    act.wait_ge(rn_done, BATCH * (s.n + 1))
                    nc.scalar.activation(of_step(normed, s), rn[s.par][:, :], ACT.Copy).then_inc(rows_kept, 1)
                    route_copy(STEPS + s.n, s.par)

            for r in range(STEPS):
                route_copy(r, r % 2)
            act.wait_ge(wg_ready, 1)
            nc.scalar.activation(wg_sb[:, :], bank[7][:, 0:D], ACT.Copy).then_inc(wg_copied, 1)
            expert_unit(0)
            expert_unit(1)
            act.wait_ge(attn_w_loaded, 16 * 6)
            rolled(act, attention, -2, 2, STEPS - 2, STEPS + 2)
            expert_unit(2)
            expert_unit(3)

        @block.vector
        def _(dve):
            NEWTON = 3
            SMALL = 5 + 3 * NEWTON

            def tile_stats(col, src, tiles=BATCH):
                for b in range(tiles):
                    last = nc.vector.bn_stats(st[:, col + b, :], src(b))
                return last

            def small(i, lo, hi, par, chain, base, ready):
                c = slice(lo, hi)
                stt = nc.vector.scalar_tensor_tensor
                dve.wait_ge(chain, base + i + 1)
                if i == 0:
                    nc.vector.tensor_tensor(mean2[:, c], st[:, c, 1], st[:, c, 4], ALU.add)
                    nc.vector.tensor_tensor(var[:, c], st[:, c, 2], st[:, c, 5], ALU.add)
                    ins = nc.vector.tensor_tensor(tt[:, c], st[:, c, 1], st[:, c, 4], ALU.subtract)
                elif i == 1:
                    ins = nc.vector.tensor_tensor(uu[:, c], tt[:, c], tt[:, c], ALU.mult)
                elif i == 2:
                    ins = stt(out=uu[:, c], in0=var[:, c], scalar=4.0 / D, in1=uu[:, c], op0=ALU.mult, op1=ALU.add)
                elif i == 3:
                    ins = nc.vector.tensor_scalar(var[:, c], uu[:, c], 0.25, EPS, ALU.mult, ALU.add)
                elif i == 4:
                    ins = nc.vector.tensor_scalar(yy[:, c].bitcast(I32), var[:, c].bitcast(I32), -0.5, RSQRT_MAGIC,
                                                  ALU.mult, ALU.add)
                elif i == SMALL:
                    stt(out=shift[par][:, c], in0=mean2[:, c], scalar=-0.5, in1=rstd[par][:, c],
                        op0=ALU.mult, op1=ALU.mult).then_inc(ready, 1)
                    return
                elif (i - 5) % 3 == 0:
                    ins = nc.vector.tensor_tensor(tt[:, c], yy[:, c], yy[:, c], ALU.mult)
                elif (i - 5) % 3 == 1:
                    ins = stt(out=uu[:, c], in0=tt[:, c], scalar=-0.5, in1=var[:, c], op0=ALU.mult, op1=ALU.mult)
                else:
                    dst = rstd[par] if i == SMALL - 1 else yy
                    ins = stt(out=dst[:, c], in0=uu[:, c], scalar=1.5, in1=yy[:, c], op0=ALU.add, op1=ALU.mult)
                ins.then_inc(chain, 1)

            def route_front(g):
                dve.wait_ge(x_loaded[g], 16 * BATCH)
                tile = lambda t: slice((g * GROUP_TILES + t) * D, (g * GROUP_TILES + t + 1) * D)
                tile_stats(0, lambda t: res[:, tile(t)], GROUP_TILES).then_inc(ln_chain0[g], 1)
                for i in range(SMALL + 1):
                    small(i, 0, GROUP_TILES, g, ln_chain0[g], 0, ln_chain0[g])
                dve.wait_ge(ln_chain0[g], SMALL + 2)
                for t in range(GROUP_TILES):
                    ins = nc.vector.tensor_scalar(normed[:, tile(t)], res[:, tile(t)], rstd[g][:, t:t + 1],
                                                  shift[g][:, t:t + 1], ALU.mult, ALU.add)
                    if t % BATCH == BATCH - 1:
                        ins.then_inc(rows_kept, 1)

            def add_router_bias(r, step_of):
                dve.wait_ge(logits_ready, r + 1)
                n = BATCH * EXPERTS
                nc.vector.tensor_tensor(
                    logits[:, bass.ds(step_of * n, n)].rearrange("p (b e) -> p b e", e=EXPERTS),
                    bank[4][:, 0:n].rearrange("p (b e) -> p b e", e=EXPERTS),
                    br_sb[:, :].unsqueeze(1).to_broadcast([P, BATCH, EXPERTS]), ALU.add).then_inc(logits_added, 1)

            def route(u):
                chain = Chain(dve, route_chain[u])
                dve.wait_ge(logits_added, (u + 1) * GROUP_STEPS)
                g, n = u % GROUPS, GROUP_TILES * EXPERTS
                by_tile = lambda t: t.rearrange("p (i e) -> p i e", e=EXPERTS)
                as_tile = lambda t: t[:, :].rearrange("p (e i) -> p i e", e=EXPERTS)
                by_expert = lambda t: t[:, :].rearrange("p (e i) -> p e i", e=EXPERTS)
                spread = lambda t: t[:, :].unsqueeze(2).to_broadcast([P, GROUP_TILES, EXPERTS])
                lg, pk = by_tile(logits[:, g * n:(g + 1) * n]), by_tile(pick[:, :])
                chain.link(nc.vector.tensor_reduce(best[:, :], lg, AX_X, ALU.max))
                chain.link(nc.vector.tensor_tensor(pk, lg, spread(best), ALU.is_equal))
                chain.link(nc.vector.tensor_tensor(pk, pk, cst("prefer").unsqueeze(1).to_broadcast(
                    [P, GROUP_TILES, EXPERTS]), ALU.mult))
                chain.link(nc.vector.tensor_reduce(best[:, :], pk, AX_X, ALU.max))
                chain.link(nc.vector.tensor_tensor(as_tile(onehot), pk, spread(best), ALU.is_equal))
                nc.vector.tensor_copy(onehot_bf[:, :], onehot[:, :]).then_inc(onehot_ready[u], 1)
                dve.wait_ge(counts_ready[u], 1)
                chain.link(nc.vector.tensor_copy(total[:, :], bank[6][:, 0:n]))
                chain.link(nc.vector.tensor_tensor_scan(upto[:, :], cst("not_first"), total[:, :], 0.0, ALU.mult, ALU.add))
                chain.link(nc.vector.tensor_scalar(tiles_e[:, :], by_expert(upto)[:, :, GROUP_TILES - 1], P / 2 - 0.5,
                                                   1.0 / P, ALU.add, ALU.mult))
                chain.link(nc.vector.tensor_scalar(tiles_e[:, :], tiles_e[:, :], ROUND, -ROUND, ALU.add, ALU.add))
                chain.link(nc.vector.tensor_tensor_scan(ends_e[:, :], cst("ones")[:, 0:EXPERTS], tiles_e[:, :], 0.0,
                                                        ALU.mult, ALU.add))
                nc.vector.tensor_tensor(base_e[:, :], ends_e[:, :], tiles_e[:, :], ALU.subtract)
                chain.link(nc.vector.tensor_tensor(place[:, :], bank[5][:, 0:n], upto[:, :], ALU.add))
                chain.link(nc.vector.tensor_tensor(place[:, :], place[:, :], total[:, :], ALU.subtract))
                chain.link(nc.vector.scalar_tensor_tensor(out=by_expert(place), in0=base_e[:, :].unsqueeze(2).to_broadcast(
                    [P, EXPERTS, GROUP_TILES]), scalar=float(P), in1=by_expert(place), op0=ALU.mult, op1=ALU.add))
                chain.link(nc.vector.tensor_tensor(place[:, :], place[:, :], onehot[:, :], ALU.mult))
                chain.link(nc.vector.tensor_reduce(slot_of_f[:, :], as_tile(place), AX_X, ALU.add))
                nc.vector.tensor_copy(slot_of[u][:, :], slot_of_f[:, :]).then_inc(slots_known[u], 1)
                ended_v = ended[:, :].rearrange("p (j e) -> p j e", e=EXPERTS)
                chain.link(nc.vector.tensor_tensor(ended_v, ends_e[0:1, :].unsqueeze(1).to_broadcast([1, SLOT_TILES, EXPERTS]),
                                                   cst("slot_tile", 1).unsqueeze(2).to_broadcast([1, SLOT_TILES, EXPERTS]),
                                                   ALU.is_le))
                chain.link(nc.vector.tensor_reduce(owner_f[:, :], ended_v, AX_X, ALU.add))
                nc.vector.tensor_scalar(owner[u][:, :], owner_f[:, :], float(EXPERTS - 1), None,
                                        ALU.min).then_inc(owners_known[u], 1)

            def expert_unit(u):
                def load_expert(t):
                    return dve.value_load(owner[u][0:1, bass.ds(t, 1)], min_val=0, max_val=EXPERTS - 1)

                def add_b1(t, par, e):
                    dve.wait_ge(up_done[u], t + 1)
                    wait(dve, hT_ready[u], t - 1)
                    nc.vector.tensor_tensor(h_pre[par][:, :], bank[2 + par][:, :], b1_sb[:, bass.ds(e * FF, FF)],
                                            ALU.add).then_inc(b1_added[u], 1)

                def add_b2(t, par, e):
                    dve.wait_ge(down_done[u], t + 1)
                    nc.vector.scalar_tensor_tensor(out=slot_y[:, bass.ds(t * D, D)], in0=bank[6 + par][:, 0:D], scalar=0.5,
                                                   in1=b2_sb[:, bass.ds(e * D, D)], op0=ALU.mult,
                                                   op1=ALU.add).then_inc(b2_added[u], 1)

                def sums(k, it=0):
                    if k < SLOT_TILES:
                        e = load_expert(2 * it + k)
                    if k >= 2:
                        e2 = load_expert(2 * it + k - 2)
                    if k < SLOT_TILES:
                        add_b1(2 * it + k, k % 2, e)
                    if k >= 2:
                        add_b2(2 * it + k - 2, k % 2, e2)

                dve.wait_ge(owners_known[u], 1)
                if u % GROUPS:
                    dve.wait_ge(y_stored[u - 1], 16 * SLOT_TILES)
                    dve.wait_ge(hT_ready[u - 1], SLOT_TILES)
                rolled(dve, sums, 0, 4, SLOT_TILES, SLOT_TILES + 2)

            def front(s):
                dve.wait_ge(qkv_done, BATCH * (s.n + 1))
                wait(dve, delta_ready, s.n - 1)
                k_ = qkv[s.par][:, :].rearrange("p (b w) -> p b w", b=BATCH)[:, :, D:2 * D]
                nc.vector.tensor_tensor(per_batch(kd[s.par][:, :]), k_,
                                        cst("decay_k").unsqueeze(1).to_broadcast([P, BATCH, D]),
                                        ALU.mult).then_inc(kd_done, 1)
                dve.wait_ge(qT_ready, s.n + 1)
                wait(dve, inter_ready, s.n - 1)
                nc.vector.tensor_tensor(per_batch(qdT[s.par][:, :]), per_batch(bank[5][:, :]),
                                        cst("decay_q").unsqueeze(1).to_broadcast([P, BATCH, P]),
                                        ALU.mult).then_inc(qdT_done, 1)

            def times_q(s, h):
                q_ = qkv[s.par][:, :].rearrange("p (b w) -> p b w", b=BATCH)
                wait(dve, o_in_done, PAIRS * s.n + h - 2)
                dve.wait_ge(state_ready, PAIRS * s.n + h + 1)
                q2 = q_[:, :, h * 2 * HD:(h + 1) * 2 * HD].unsqueeze(3).to_broadcast([P, BATCH, 2 * HD, HD])
                nc.vector.tensor_tensor(qS[h % 3][:, :].rearrange("p (b a e) -> p b a e", b=BATCH, e=HD),
                                        bank[h % 3][:, :].rearrange("p (b a e) -> p b a e", b=BATCH, e=HD),
                                        q2, ALU.mult).then_inc(qS_done, 1)

            def sum_d(s, h):
                dve.wait_ge(qS_done, PAIRS * s.n + h + 1)
                w = BATCH * 2 * HD
                nc.vector.tensor_reduce(o_in[:, h * w:(h + 1) * w].rearrange("p (a e) -> p a e", e=HD),
                                        qS[h % 3][:, :].rearrange("p (a d e) -> p a e d", d=HD, e=HD),
                                        AX_X, ALU.add).then_inc(o_in_done, 1)

            def join(s):
                dve.wait_ge(inter_ready, s.n + 1)
                dve.wait_ge(o_in_done, PAIRS * (s.n + 1))
                wait(dve, on_done, BATCH * s.n)
                w2 = 2 * HD
                nc.vector.tensor_tensor(
                    o_all[:, :].rearrange("p (b h w) -> p b h w", b=BATCH, w=w2),
                    bank[7][:, :].rearrange("p (b h w) -> p b h w", b=BATCH, w=w2),
                    o_in[:, :].rearrange("p (h b w) -> p b h w", b=BATCH, w=w2), ALU.add).then_inc(o_done, 1)

            def mask_delta(s):
                dve.wait_ge(delta_ready, s.n + 1)
                nc.vector.tensor_tensor(per_batch(carry_new[:, :]), per_batch(bank[6][:, :]),
                                        cst("carry_mask").unsqueeze(1).to_broadcast([P, BATCH, D]),
                                        ALU.mult).then_inc(delta_masked, 1)

            def update_carry(s):
                dve.wait_ge(delta_masked, s.n + 1)
                nc.vector.scalar_tensor_tensor(out=carry[:, :], in0=carry[:, :], scalar=cst("decay_c"), in1=carry_new[:, :],
                                               op0=ALU.mult, op1=ALU.add).then_inc(carry_done, 1)

            def gate(s):
                dve.wait_ge(onT_copied, s.n + 1)
                dve.wait_ge(gate_done, s.n + 1)
                wait(dve, wo_ready, s.n)
                nc.vector.scalar_tensor_tensor(out=o_gT[:, :], in0=gateT[s.par][:, :], scalar=1.0, in1=o_nT[:, :],
                                               op0=ALU.add, op1=ALU.mult).then_inc(gated, 1)

            def residual(s):
                dve.wait_ge(wo_ready, s.n + 1)
                nc.vector.scalar_tensor_tensor(out=of_step(res, s), in0=bank[7][:, :], scalar=0.5, in1=of_step(res, s),
                                               op0=ALU.mult, op1=ALU.add).then_inc(res_done, 1)

            def attention(k, it=0):
                here = step(k, it)
                base = (here.n + 2) * (SMALL + 1)
                res_tile = lambda s: lambda b: res[:, bass.ds(s.n * BATCH * D + b * D, D)]
                cols = []
                if k >= 2:
                    old = step(k - 2, it)
                    dve.wait_ge(res_done, old.n + 1)
                    last = tile_stats(ROUTED, res_tile(old))
                    cols.append(ROUTED)
                if k + 2 < STEPS:
                    last = tile_stats(AHEAD, res_tile(step(k + 2, it)))
                    cols.append(AHEAD)
                if 1 <= k <= STEPS:
                    dve.wait_ge(o_done, here.n)
                    last = tile_stats(OUTPUT, lambda b: o_all[:, b * D:(b + 1) * D])
                    cols.append(OUTPUT)
                last.then_inc(ln_chain, 1)
                todo = iter(range(SMALL + 1))
                lo, hi = min(cols), max(cols) + BATCH

                def small_steps(count):
                    for _, i in zip(range(count), todo):
                        small(i, lo, hi, here.par, ln_chain, base, ln_ready)

                if 0 <= k < STEPS:
                    times_q(here, 0)
                    for h in range(PAIRS):
                        small_steps(1)
                        if h + 1 < PAIRS:
                            times_q(here, h + 1)
                        small_steps(1)
                        sum_d(here, h)
                small_steps(SMALL + 1)
                if 0 <= k + 1 < STEPS:
                    front(step(k + 1, it))
                if 0 <= k < STEPS:
                    mask_delta(here)
                    join(here)
                    update_carry(here)
                if 1 <= k <= STEPS:
                    gate(step(k - 1, it))
                    residual(step(k - 1, it))
                if k >= 2:
                    old = step(k - 2, it)
                    add_router_bias(STEPS + old.n, old.n)

            dve.wait_ge(const_loaded, 16)
            nc.vector.tensor_copy(upper_bf[:, :], cst("upper"))
            nc.vector.tensor_copy(ones_bf[:, :], cst("ones")).then_inc(bf_ready, 1)
            nc.vector.memset(carry[:, :], 0.0).then_inc(carry_done, 1)
            dve.wait_ge(router_loaded, 32)
            for g in range(GROUPS):
                route_front(g)
                for r in range(g * GROUP_STEPS, (g + 1) * GROUP_STEPS):
                    add_router_bias(r, r)
                route(g)
            dve.wait_ge(expert_w_loaded, 64)
            nc.vector.tensor_scalar(b2_sb[:, :], b2_sb[:, :], 0.5, None, ALU.mult).then_inc(b2_halved, 1)
            dve.wait_ge(b2_halved, 1)
            expert_unit(0)
            expert_unit(1)
            dve.wait_ge(fetched[0], 16 * GROUP_TILES)
            for k in range(-2, 2):
                attention(k)
            dve.wait_ge(fetched[1], 16 * GROUP_TILES)
            rolled(dve, attention, 2, 2, STEPS - 2, STEPS - 2)
            route(2)
            for k in range(STEPS - 2, STEPS + 2):
                attention(k)
            route(3)
            expert_unit(2)
            expert_unit(3)

        @block.tensor
        def _(pe):
            mm = nc.tensor.matmul

            def transpose4(dst, src, done):
                for b in range(BATCH):
                    last = nc.tensor.transpose(dst[:, b * P:(b + 1) * P], src(b), ident)
                last.then_inc(done, 1)

            def route_product(r, par):
                pe.wait_ge(rnT_copied, r + 1)
                wait(pe, logits_added, r)
                for b in range(BATCH):
                    last = mm(bank[4][:, b * EXPERTS:(b + 1) * EXPERTS], rnT[par][:, b * P:(b + 1) * P], wr_sb[:, :],
                              start=True, stop=True)
                last.then_inc(logits_ready, 1)

            def route_counts(u):
                pe.wait_ge(onehot_ready[u], 1)
                if u > 0:
                    pe.wait_ge(slots_known[u - 1], 1)
                n = GROUP_TILES * EXPERTS
                mm(bank[5][:, 0:n], upper_bf[:, :], onehot_bf[:, :], start=True, stop=True)
                mm(bank[6][:, 0:n], ones_bf[:, :], onehot_bf[:, :], start=True, stop=True).then_inc(counts_ready[u], 1)

            def expert_unit(u):
                def load_expert(t):
                    return pe.value_load(owner[u][0:1, bass.ds(t, 1)], min_val=0, max_val=EXPERTS - 1)

                def slot_transpose(s):
                    pe.wait_ge(slot_loaded[u][s.par], 16 * (s.half + 1))
                    wait(pe, slotT_copied[u], s.n - 1)
                    nc.tensor.transpose(bank[s.par][:, 0:P], slot_x[s.par], ident).then_inc(slotT_ready[u], 1)

                def up(s, e):
                    pe.wait_ge(slotT_copied[u], s.n + 1)
                    wait(pe, b1_added[u], s.n - 1)
                    mm(bank[2 + s.par][:, :], slotT[s.par], w1_sb[:, bass.ds(e * FF, FF)],
                       start=True, stop=True).then_inc(up_done[u], 1)

                def h_transpose(s):
                    pe.wait_ge(b1_added[u], s.n + 1)
                    wait(pe, hT_copied[u], s.n - 1)
                    for f in range(FB):
                        last = nc.tensor.transpose(bank[4 + s.par][:, f * P:(f + 1) * P],
                                                   h_pre[s.par][:, f * P:(f + 1) * P], ident)
                    last.then_inc(hT_ready[u], 1)

                def down(s, e):
                    pe.wait_ge(hT_copied[u], s.n + 1)
                    wait(pe, b2_added[u], s.n - 1)
                    for f in range(FB):
                        last = mm(bank[6 + s.par][:, 0:D], h_T[s.par][:, f * P:(f + 1) * P],
                                  w2_sb[:, bass.ds(e * FF + f * D, D)], start=(f == 0), stop=(f == FB - 1))
                    last.then_inc(down_done[u], 1)

                def stages(k, it=0):
                    if 0 <= k < SLOT_TILES:
                        e_up = load_expert(step(k, it).n)
                    if 0 <= k - 2:
                        e_down = load_expert(step(k - 2, it).n)
                    if k + 1 < SLOT_TILES:
                        slot_transpose(step(k + 1, it))
                    if 0 <= k < SLOT_TILES:
                        up(step(k, it), e_up)
                    if 0 <= k - 1 < SLOT_TILES:
                        h_transpose(step(k - 1, it))
                    if 0 <= k - 2:
                        down(step(k - 2, it), e_down)

                pe.wait_ge(owners_known[u], 1)
                if u % GROUPS:
                    pe.wait_ge(hT_copied[u - 1], SLOT_TILES)
                    pe.wait_ge(b2_added[u - 1], SLOT_TILES)
                rolled(pe, stages, -1, 4, SLOT_TILES - 1, SLOT_TILES + 2)

            def norm_transpose(s):
                pe.wait_ge(xn_done, BATCH * (s.n + 1))
                wait(pe, qdT_done, s.n)
                wait(pe, onT_copied, s.n - 2)
                transpose4(bank[5], lambda b: xn[s.par][:, b * D:(b + 1) * D], xnT_ready)

            def project(s, b):
                pe.wait_ge(xnT_copied, s.n + 1)
                wait(pe, qkv_done, BATCH * s.n + b - 1)
                if b == 0:
                    pe.wait_ge(rnT_copied, STEPS + s.n - 3)
                if b == 1:
                    pe.wait_ge(logits_added, STEPS + s.n - 3)
                mm(bank[3 + b % 2][:, 0:3 * D], xnT[s.par][:, b * P:(b + 1) * P], wqkv_sb[:, :],
                   start=True, stop=True).then_inc(qkv_ready, 1)

            def gate_product(s):
                wait(pe, delta_masked, s.n)
                mm(bank[6][:, :], wg_sb[:, :], xnT[s.par][:, :], start=True, stop=True).then_inc(gate_ready, 1)

            def state_product(s, h):
                pe.wait_ge(outer_done, 2 * s.n + 1 + h // (PAIRS // 2))
                before = PAIRS * s.n + h - 3 if h >= 3 else PAIRS * (s.n - 1) + 6 + h if h < 2 else PAIRS * (s.n - 1) + 5
                wait(pe, qS_done, before + 1)
                for a in range(2):
                    u = outer[s.par][:, :].rearrange("p (b w) -> p b w", b=BATCH)[:, :, (2 * h + a) * UH:(2 * h + a + 1) * UH]
                    to = bank[h % 3][:, :].rearrange("p (b a w) -> p b a w", b=BATCH, a=2)[:, :, a, :]
                    last = mm(to, decay_sb[:, (2 * h + a) * P:(2 * h + a + 1) * P], u, start=True, stop=True)
                last.then_inc(state_ready, 1)

            def inter_product(s):
                pe.wait_ge(qdT_done, s.n + 1)
                pe.wait_ge(carry_done, s.n + 1)
                wait(pe, res_done, s.n - 1)
                for b in range(BATCH):
                    last = mm(bank[7][:, b * D:(b + 1) * D], qdT[s.par][:, b * P:(b + 1) * P], carry[:, b * D:(b + 1) * D],
                              start=True, stop=True)
                last.then_inc(inter_ready, 1)

            def carry_product(s):
                pe.wait_ge(kd_done, s.n + 1)
                pe.wait_ge(gate_done, s.n + 1)
                for b in range(BATCH):
                    v_ = qkv[s.par][:, b * 3 * D + 2 * D:(b + 1) * 3 * D]
                    last = mm(bank[6][:, b * D:(b + 1) * D], kd[s.par][:, b * D:(b + 1) * D], v_, start=True, stop=True)
                last.then_inc(delta_ready, 1)

            def q_transpose(s):
                pe.wait_ge(qkv_done, BATCH * (s.n + 1))
                transpose4(bank[5], lambda b: qkv[s.par][:, b * 3 * D:b * 3 * D + D], qT_ready)

            def out_transpose(s, k):
                pe.wait_ge(on_done, BATCH * (s.n + 1))
                pe.wait_ge(qdT_done, s.n + 3 if k + 1 < STEPS else STEPS)
                transpose4(bank[5], lambda b: o_n[:, b * D:(b + 1) * D], onT_ready)

            def out_product(s, k):
                pe.wait_ge(gated, s.n + 1)
                pe.wait_ge(o_done, s.n + 2 if k < STEPS else STEPS)
                for b in range(BATCH):
                    last = mm(bank[7][:, b * D:(b + 1) * D], o_gT[:, b * P:(b + 1) * P], wo_sb[:, :], start=True, stop=True)
                last.then_inc(wo_ready, 1)

            def route_transpose(s):
                pe.wait_ge(rn_done, BATCH * (s.n + 1))
                pe.wait_ge(rnT_copied, STEPS + s.n)
                transpose4(bank[3], lambda b: rn[s.par][:, b * D:(b + 1) * D], rnT_ready)

            def attention(k, it=0):
                cur, nxt = step(k, it), step(k + 1, it)
                has_cur, has_nxt = 0 <= k < STEPS, 0 <= k + 1 < STEPS
                if has_nxt:
                    norm_transpose(nxt)
                for h in range(PAIRS):
                    if has_cur:
                        state_product(cur, h)
                    if has_nxt and h < BATCH:
                        project(nxt, h)
                    if has_cur and h == BATCH:
                        gate_product(cur)
                if has_nxt:
                    q_transpose(nxt)
                if has_cur:
                    inter_product(cur)
                    carry_product(cur)
                if 1 <= k <= STEPS:
                    out_transpose(step(k - 1, it), k)
                if k >= 2:
                    route_transpose(step(k - 2, it))
                if 1 <= k <= STEPS:
                    out_product(step(k - 1, it), k)
                if k >= 2:
                    old = step(k - 2, it)
                    route_product(STEPS + old.n, old.par)

            pe.wait_ge(const_loaded, 16)
            pe.wait_ge(router_loaded, 32)
            for g in range(GROUPS):
                for k in range(GROUP_STEPS + 1):
                    r = g * GROUP_STEPS + k
                    if k < GROUP_STEPS:
                        pe.wait_ge(rows_kept, r + 1)
                        wait(pe, rnT_copied, r)
                        transpose4(bank[3], lambda b: normed[:, (r * BATCH + b) * D:(r * BATCH + b + 1) * D], rnT_ready)
                    if k >= 1:
                        route_product(r - 1, (r - 1) % 2)
                pe.wait_ge(bf_ready, 1)
                route_counts(g)
            pe.wait_ge(attn_w_loaded, 16 * 6)
            mm(bank[7][:, 0:D], wg1_sb[:, :], wg2_sb[:, :], start=True, stop=True).then_inc(wg_ready, 1)
            pe.wait_ge(expert_w_loaded, 64)
            pe.wait_ge(wg_copied, 1)
            expert_unit(0)
            expert_unit(1)
            pe.wait_ge(decay_loaded, 16)
            rolled(pe, attention, -1, 2, STEPS - 2, STEPS - 2)
            pe.wait_ge(delta_masked, STEPS - 2)
            pe.wait_ge(onT_copied, STEPS - 3)
            route_counts(2)
            pe.wait_ge(slots_known[2], 1)
            for k in range(STEPS - 2, STEPS + 2):
                attention(k)
            pe.wait_ge(delta_masked, STEPS)
            pe.wait_ge(onT_copied, STEPS)
            route_counts(3)
            expert_unit(2)
            expert_unit(3)


def head_slopes():
    start = 2.0 ** (-2.0 ** (-(np.log2(HEADS) - 3)))
    s = np.array([start * start ** i for i in range(HEADS)], dtype=np.float32)
    return (s * np.float32(1.0 + 1e-05)).astype(np.float64)


def constants():
    s, i = head_slopes(), np.arange(P, dtype=np.float64)
    diff = i[None, :] - i[:, None]
    decay = np.where(diff >= 0, np.exp(-s[:, None, None] * np.maximum(diff, 0)), 0.0)
    per_row = np.repeat(s, HD)
    head = np.arange(P) // HD
    parts = {
        "ident": np.eye(P),
        "carry_mask": head[:, None] == head[None, :],
        "decay_q": np.exp(-per_row[:, None] * (i[None, :] + 1)),
        "decay_k": np.exp(-per_row[None, :] * (P - 1 - i[:, None])),
        "decay_c": np.exp(-per_row[:, None] * P),
        "upper": diff > 0,
        "ones": np.ones((P, P)),
        "not_first": np.tile((np.arange(EXPERTS * GROUP_TILES) % GROUP_TILES != 0)[None, :], (P, 1)),
        "prefer": np.tile((EXPERTS - np.arange(EXPERTS))[None, :], (P, 1)),
        "slot_tile": np.tile(np.arange(SLOT_TILES)[None, :], (P, 1)),
    }
    const = np.concatenate([np.asarray(parts[n], dtype=np.float64) for n in CONST], axis=1).astype(np.float32)
    return decay.transpose(1, 0, 2).reshape(P, HEADS * P).astype(np.float32), const


def kernel(**inputs):
    import concourse.bacc as bacc
    from concourse.bass_utils import run_bass_kernel_spmd

    a = {k: np.asarray(v) for k, v in inputs.items()}
    decay, const = constants()
    w2 = a["L0_ffn_W2"].reshape(EXPERTS, D, FB, P)
    arrays = {
        "x": a["L0_attn_x"].reshape(BATCH * SEQ, D),
        "w1t": a["L0_ffn_W1"].transpose(2, 0, 1).reshape(D, EXPERTS * FF),
        "b1": a["L0_ffn_b1"].reshape(EXPERTS * FF),
        "w2t": w2.transpose(3, 0, 2, 1).reshape(P, EXPERTS * FB * D),
        "b2": a["L0_ffn_b2"].reshape(EXPERTS * D),
        "wrt": a["L0_ffn_Wr"].T,
        "br": a["L0_ffn_br"],
        "wqkv": np.concatenate([a["L0_attn_Wq"], a["L0_attn_Wk"], a["L0_attn_Wv"]], axis=1),
        "wg1t": a["L0_attn_Wg1"].T,
        "wg2": a["L0_attn_Wg2"],
        "wo": a["L0_attn_Wo"],
        "gamma": a["L0_attn_gamma"].reshape(D, 1),
        "beta": a["L0_attn_beta"].reshape(D, 1),
        "decay": decay,
        "const": const,
    }
    nc = bacc.Bacc("TRN2", target_bir_lowering=False, num_devices=1)
    arrays = {f"in_{k}": np.ascontiguousarray(v) for k, v in arrays.items()}
    args = [nc.dram_tensor(k, v.shape, mybir.dt.from_np(v.dtype), kind="ExternalInput").ap() for k, v in arrays.items()]
    out = nc.dram_tensor("out_x", (BATCH * SEQ, D), F32, kind="ExternalOutput").ap()
    build(nc, *args, out)
    r = run_bass_kernel_spmd(nc, [arrays], core_ids=[0])
    return r.results[0]["out_x"].reshape(BATCH, SEQ, D)
```

```python
from collections import namedtuple
from contextlib import ExitStack

import numpy as np

import concourse.bass as bass
from concourse import mybir

F32 = mybir.dt.float32
F32R = mybir.dt.float32r
BF16 = mybir.dt.bfloat16
I32 = mybir.dt.int32
ALU = mybir.AluOpType
ACT = mybir.ActivationFunctionType
AX_X = mybir.AxisListType.X

P = 128
BATCH, SEQ, D = 4, 1024, 128
STEPS = SEQ // P
TOKEN_TILES = BATCH * STEPS
EXPERTS, FF = 8, 512
FB = FF // P
GROUPS = 2
GROUP_STEPS = STEPS // GROUPS
GROUP_TILES = TOKEN_TILES // GROUPS
SLOT_TILES = GROUP_TILES + EXPERTS - 1
LAYER_TILES = GROUPS * SLOT_TILES
LAYERS = 2
UNITS = LAYERS * GROUPS
NO_TOKEN = BATCH * SEQ
HEADS = 16
HD = D // HEADS
PAIRS = HEADS // 2
UH = HD * HD
UW = HEADS * UH
EPS = 1e-5
ROUND = 1.5 * 2.0 ** 23
RSQRT_MAGIC = float(0x5F3759DF + 0x00800000)
ROOT_3_8 = float(np.sqrt(3 / 8))

CONST = {}
_at = 0
for _name, _width in (("ident", P), ("carry_mask", P), ("decay_q", P), ("decay_k", P), ("decay_c", 1),
                      ("upper", P), ("ones", P), ("not_first", EXPERTS * GROUP_TILES),
                      ("prefer", EXPERTS), ("slot_tile", SLOT_TILES), ("token", TOKEN_TILES)):
    CONST[_name] = (_at, _width)
    _at += _width
CONST_W = _at

Step = namedtuple("Step", "n par")
Slot = namedtuple("Slot", "n round buf par")
SLOT_BUFS = 4
ROLL = 2 * SLOT_BUFS
BIAS_W = FF + D


def step(k):
    return Step(k, k % 2)


def slot(k, it=0):
    return Slot(ROLL * it + k, ROLL // SLOT_BUFS * it + k // SLOT_BUFS, k % SLOT_BUFS, k % 2)


def wait(eng, sem, value):
    if isinstance(value, int) and value <= 0:
        return
    eng.wait_ge(sem, value)


def rolled(eng, body, first, loop_from, loop_to, end, by=2, edge=lambda: None):
    rounds = (loop_to - loop_from) // by
    for k in range(first, loop_from):
        body(k)
    if rounds:
        with eng.Fori(0, rounds) as it:
            edge()
            for k in range(loop_from, loop_from + by):
                body(k, it)
        edge()
    for k in range(loop_from + rounds * by, end):
        body(k)


class Experts:

    def __init__(self, eng, owner, most):
        self.eng, self.owner, self.most, self.regs = eng, owner, most, {}

    def forget(self):
        self.regs = {}

    def of(self, s, k):
        if k not in self.regs:
            self.regs[k] = self.eng.value_load(self.owner[0:1, bass.ds(s.n, 1)], min_val=0, max_val=self.most)
        return self.regs[k]


class Chain:

    def __init__(self, eng, sem):
        self.eng, self.sem, self.k = eng, sem, 0

    def link(self, ins):
        self.k += 1
        ins.then_inc(self.sem, 1)
        self.eng.wait_ge(self.sem, self.k)


def build(nc, x, w1t, bias, w2t, wrt, br, wqkv, wg1t, wg2, wo, gamma, beta, decay, const, out):
    with ExitStack() as ctx:
        def sb(name, shape, dt=F32):
            return ctx.enter_context(nc.sbuf_tensor(name, shape, dt))

        def pb(name, shape=(P, 512)):
            return ctx.enter_context(nc.psum_tensor(name, list(shape), F32))

        def sem(name):
            return ctx.enter_context(nc.semaphore(name))

        def by_slot(name, width, dt):
            return [nc.dram_tensor(f"{name}{g}", (SLOT_TILES * P, width), dt, kind="Internal").ap() for g in range(GROUPS)]

        slots_in, slots_out, slot_tokens = by_slot("slots_in", D, F32), by_slot("slots_out", D, F32), by_slot("slot_tokens", 1, I32)

        res = sb("res", [P, TOKEN_TILES * D])
        normed = sb("normed", [P, TOKEN_TILES * D])
        w1_hi, w1_lo = sb("w1_hi", [P, EXPERTS * FF], F32R), sb("w1_lo", [P, EXPERTS * FF], F32R)
        w2_sb = sb("w2_sb", [P, EXPERTS * FF])
        biases = sb("biases", [P, EXPERTS * BIAS_W])
        decay_sb = sb("decay_sb", [P, HEADS * P])
        const_sb = sb("const_sb", [P, CONST_W])
        wr_sb = sb("wr_sb", [P, EXPERTS])
        br_sb = sb("br_sb", [P, EXPERTS])
        wqkv_sb = sb("wqkv_sb", [P, 3 * D])
        wo_sb = sb("wo_sb", [P, D])
        wg_sb = sb("wg_sb", [P, D])
        gb_sb = sb("gb_sb", [P, 2])
        upper_bf = sb("upper_bf", [P, P], BF16)
        ones_bf = sb("ones_bf", [P, P], BF16)

        xn = sb("xn", [P, BATCH * D])
        xnT = [sb(f"xnT{i}", [P, BATCH * P]) for i in range(2)]
        rnT = [sb(f"rnT{i}", [P, BATCH * P]) for i in range(2)]
        qkv = [sb(f"qkv{i}", [P, BATCH * 3 * D]) for i in range(2)]
        gateT = [sb(f"gateT{i}", [P, BATCH * P]) for i in range(2)]
        outer_all = sb("outer_all", [P, 2 * BATCH * UW])
        outer = [outer_all[:, i * BATCH * UW:(i + 1) * BATCH * UW] for i in range(2)]
        zeros = outer_all[:, 0:SLOT_TILES * D]
        w1_raw = outer_all[:, BATCH * UW:BATCH * UW + EXPERTS * FF]
        slot_y = outer_all[:, 0:LAYER_TILES * D]
        kd = [sb(f"kd{i}", [P, BATCH * D]) for i in range(2)]
        qdT = [sb(f"qdT{i}", [P, BATCH * P]) for i in range(2)]
        qS = [sb(f"qS{i}", [P, 512]) for i in range(3)]
        o_in = sb("o_in", [P, BATCH * D])
        o_all = sb("o_all", [P, BATCH * D])
        o_n = sb("o_n", [P, BATCH * D])
        o_nT = sb("o_nT", [P, BATCH * P])
        o_gT = sb("o_gT", [P, BATCH * P])
        wg1_sb, wg2_sb = o_gT[0:HD, 0:D], o_gT[0:HD, D:2 * D]
        carry = sb("carry", [P, BATCH * D])
        carry_new = sb("carry_new", [P, BATCH * D])
        h_pre, h_T = kd, qdT
        slot_x = [carry[:, i * D:(i + 1) * D] for i in range(SLOT_BUFS)]
        slotT_hi, slotT_lo = ([sb(f"slotT_{part}{i}", [P, P], F32R) for i in range(2)] for part in ("hi", "lo"))

        logits = sb("logits", [P, TOKEN_TILES * EXPERTS])
        onehot_bf = sb("onehot_bf", [P, GROUP_TILES * EXPERTS], BF16)
        total = sb("total", [P, GROUP_TILES * EXPERTS])
        upto = sb("upto", [P, GROUP_TILES * EXPERTS])
        place = sb("place", [P, GROUP_TILES * EXPERTS])
        pick = place
        best = sb("best", [P, GROUP_TILES])
        tiles_e = sb("tiles_e", [P, EXPERTS])
        ends_e = sb("ends_e", [P, EXPERTS])
        base_e = sb("base_e", [P, EXPERTS])
        ended = logits[0:1, 0:SLOT_TILES * EXPERTS]
        slot_of_f = sb("slot_of_f", [P, GROUP_TILES])
        owner_f = sb("owner_f", [1, SLOT_TILES])
        owner = sb("owner", [1, LAYER_TILES], I32)
        owner_bias = sb("owner_bias", [1, LAYER_TILES], I32)
        slot_of = [sb(f"slot_of{u}", [P, GROUP_TILES], I32) for u in range(UNITS)]

        token = sb("token", [P, TOKEN_TILES], I32)
        token_of = sb("token_of", [P, LAYER_TILES], I32)

        AHEAD, OUTPUT, ROUTED = 0, BATCH, 2 * BATCH
        LN_W = max(3 * BATCH, GROUP_TILES)
        st = sb("st", [P, LN_W, 6])
        mean2, var, yy, tt, uu = (sb(n, [P, LN_W]) for n in ("mean2", "var", "yy", "tt", "uu"))
        rstd = [sb(f"rstd{i}", [P, LN_W]) for i in range(2)]
        shift = [sb(f"shift{i}", [P, LN_W]) for i in range(2)]

        bank = [pb(f"bank{i}") for i in range(8)]

        def cst(name, rows=P):
            a, w = CONST[name]
            return const_sb[0:rows, a:a + w]

        ident = cst("ident")
        onehot = cst("upper")
        per_batch = lambda ap, w=D: ap.rearrange("p (b d) -> p b d", b=BATCH)
        of_step = lambda t, s: t[:, s.n * BATCH * D:(s.n + 1) * BATCH * D]

        x_loaded = [sem(f"x_loaded{c}") for c in range(STEPS)]
        const_loaded, decay_loaded = sem("const_loaded"), sem("decay_loaded")
        router_loaded, attn_w_loaded, expert_w_loaded = sem("router_loaded"), sem("attn_w_loaded"), sem("expert_w_loaded")
        zeroed, slots_cleared = sem("zeroed"), sem("slots_cleared")
        bf_ready, wg_ready, wg_copied = sem("bf_ready"), sem("wg_ready"), sem("wg_copied")
        token_ready, no_token, tokens_cleared = sem("token_ready"), sem("no_token"), sem("tokens_cleared")
        by_layer = lambda name: [sem(f"{name}{l}") for l in range(LAYERS)]
        by_unit = lambda name: [sem(f"{name}{u}") for u in range(UNITS)]
        rnT_ready, rnT_copied, rows_kept = sem("rnT_ready"), sem("rnT_copied"), sem("rows_kept")
        logits_ready, logits_added = sem("logits_ready"), sem("logits_added")
        logits_added0 = [sem(f"logits_added0_{g}") for g in range(GROUPS)]
        ln_chain0 = [sem(f"ln_chain0_{g}") for g in range(GROUPS)]
        route_chain, onehot_ready, counts_ready, counts_read, slots_known, owners_known = (
            by_unit("route_chain"), by_unit("onehot_ready"), by_unit("counts_ready"), by_unit("counts_read"),
            by_unit("slots_known"), by_unit("owners_known"))
        rows_sorted, tokens_sorted, tokens_loaded = by_unit("rows_sorted"), by_unit("tokens_sorted"), by_unit("tokens_loaded")
        fetched = [sem(f"fetched{c}") for c in range(STEPS)]
        slot_loaded = [[sem(f"slot_loaded{l}_{b}") for b in range(SLOT_BUFS)] for l in range(LAYERS)]
        slotT_split, w1_hi_done, w1_split = by_layer("slotT_split"), sem("w1_hi_done"), sem("w1_split")
        slotT_ready, slotT_copied, up_done, b1_added, hT_ready, hT_copied, down_done, b2_added = (
            by_layer("slotT_ready"), by_layer("slotT_copied"), by_layer("up_done"), by_layer("b1_added"),
            by_layer("hT_ready"), by_layer("hT_copied"), by_layer("down_done"), by_layer("b2_added"))
        y_stored = [sem(f"y_stored{g}") for g in range(GROUPS)]
        res_stored, y_scattered = [sem(f"res_stored{g}") for g in range(GROUPS)], sem("y_scattered")
        ln_chain, ln_ready, xn_done, xnT_ready, xnT_copied = (
            sem("ln_chain"), sem("ln_ready"), sem("xn_done"), sem("xnT_ready"), sem("xnT_copied"))
        qkv_ready, qkv_done, gate_ready, gate_done = sem("qkv_ready"), sem("qkv_done"), sem("gate_ready"), sem("gate_done")
        outer_done, kd_done, qT_ready, qdT_done = sem("outer_done"), sem("kd_done"), sem("qT_ready"), sem("qdT_done")
        state_ready, qS_done, o_in_done = sem("state_ready"), sem("qS_done"), sem("o_in_done")
        inter_ready, o_done, delta_ready, delta_copied, carry_done = (
            sem("inter_ready"), sem("o_done"), sem("delta_ready"), sem("delta_copied"), sem("carry_done"))
        on_done, onT_ready, onT_copied, gated, wo_ready, res_done = (
            sem("on_done"), sem("onT_ready"), sem("onT_copied"), sem("gated"),
            sem("wo_ready"), sem("res_done"))
        b2_halved, carry_aged = sem("b2_halved"), sem("carry_aged")
        delta_masked = sem("delta_masked")
        first_outer_done, table_loaded = sem("first_outer_done"), sem("table_loaded")

        WARM_ROUTING, WARM_EXPERTS = 6, [2, 2]
        W1_PIECES = 4
        TURNS = range(-1, STEPS)
        ln_turn = lambda k: max(k + 1, 0)
        LAST_RES_AT = 4
        TOKENS_AT = [1, SLOT_TILES + 7]
        EARLY_SCATTERS = 11
        ROUTE_TURN = GROUP_STEPS - 1 + 3
        slotT_bank, up_bank, hT_bank, down_bank = bank[0], bank[1], bank[2], bank[6]
        counts_bank = bank[5]
        router_bank = [bank[4], bank[7]]
        ROLL_FROM = SLOT_TILES - 3
        ROLL_END = [ROLL_FROM + 2 * ROLL, ROLL_FROM + 3 * ROLL]
        pass_edges = lambda l: range(ROLL_FROM, ROLL_END[l] + 1, ROLL)
        SMALL = 11

        def outer_product(eng, n, half, b):
            w = HEADS // 2
            at = b * 3 * D + half * w * HD
            k_ = qkv[n % 2][:, at + D:at + D + w * HD].unsqueeze(2).to_broadcast([P, w * HD, HD])
            v_ = (qkv[n % 2][:, at + 2 * D:at + 2 * D + w * HD].rearrange("p (h e) -> p h e", e=HD)
                  .unsqueeze(2).to_broadcast([P, w, HD, HD]))
            u_ = outer[n % 2][:, b * UW + half * w * UH:b * UW + (half + 1) * w * UH]
            return eng.tensor_tensor(u_.rearrange("p (h d e) -> p h d e", d=HD, e=HD),
                                     k_.rearrange("p (h d) e -> p h d e", d=HD), v_, ALU.mult)

        block = ctx.enter_context(nc.Block())

        @block.sync
        def _(sp):
            x_v = x.rearrange("(b c p) d -> p c b d", b=BATCH, p=P)
            out_v = out.rearrange("(b c p) d -> p c b d", b=BATCH, p=P)
            res_v = res[:, :].rearrange("p (c b d) -> p c b d", c=STEPS, b=BATCH)
            for c in range(STEPS):
                sp.dma_start(res_v[:, c], x_v[:, c]).then_inc(x_loaded[c], 16)
            sp.wait_ge(zeroed, 1)
            for g in range(GROUPS):
                sp.dma_start(slots_in[g].rearrange("(t p) d -> p t d", p=P),
                             zeros.rearrange("p (t d) -> p t d", d=D)).then_inc(slots_cleared, 16)
            sp.wait_ge(no_token, 1)
            for g in range(GROUPS):
                sp.dma_start(slot_tokens[g].rearrange("(p t) o -> p (t o)", p=P),
                             token_of[:, 0:SLOT_TILES]).then_inc(tokens_cleared, 16)

            AHEAD_LOADS = 5

            def experts(l):
                def load(s, g):
                    wait(sp, slotT_ready[l], s.n - SLOT_BUFS + 1)
                    sp.dma_start(slot_x[s.buf], slots_in[g][bass.ds((s.n - g * SLOT_TILES) * P, P), :]).then_inc(slot_loaded[l][s.buf], 16)

                def store(t, g):
                    sp.wait_ge(b2_added[l], t + 1)
                    sp.dma_start(slots_out[g][bass.ds((t - g * SLOT_TILES) * P, P), :],
                                 slot_y[:, bass.ds(t * D, D)]).then_inc(y_stored[g], 16)

                def load_tokens(g):
                    u = GROUPS * l + g
                    sp.wait_ge(tokens_sorted[u], 16 * GROUP_TILES)
                    sp.dma_start(token_of[:, g * SLOT_TILES:(g + 1) * SLOT_TILES],
                                 slot_tokens[g].rearrange("(t p) o -> p (t o)", p=P),
                                 allow_slow_non_contiguous=True).then_inc(tokens_loaded[u], 16)

                def move(k, it=0):
                    if l == 1 and k == LAST_RES_AT:
                        store_res(STEPS - 2)
                        store_res(STEPS - 1)
                    if l == 1 and k in TOKENS_AT:
                        load_tokens(TOKENS_AT.index(k))
                    if k + AHEAD_LOADS < LAYER_TILES:
                        load(slot(k + AHEAD_LOADS, it), int(k + AHEAD_LOADS >= SLOT_TILES))
                    if l == 0:
                        if k >= 0:
                            store(slot(k, it).n, int(k >= SLOT_TILES))

                sp.wait_ge(rows_sorted[GROUPS * l], 16 * GROUP_TILES)
                rolled(sp, move, -AHEAD_LOADS, SLOT_BUFS if l == 0 else SLOT_TILES - AHEAD_LOADS, SLOT_TILES - AHEAD_LOADS,
                       SLOT_TILES - AHEAD_LOADS, by=ROLL)
                sp.wait_ge(rows_sorted[GROUPS * l + 1], 16 * GROUP_TILES)
                rolled(sp, move, SLOT_TILES - AHEAD_LOADS, SLOT_TILES if l == 0 else TOKENS_AT[1] + 1,
                       LAYER_TILES - AHEAD_LOADS, LAYER_TILES, by=ROLL)

            experts(0)
            def store_res(c):
                sp.wait_ge(res_done, c + 1)
                sp.dma_start(out_v[:, c], res_v[:, c]).then_inc(res_stored[c // GROUP_STEPS], 16)

            for c in range(STEPS - 2):
                store_res(c)
            sp.wait_ge(inter_ready, STEPS)
            experts(1)
            sp.wait_ge(y_scattered, 16 * LAYER_TILES)

        @block.gpsimd
        def _(pool):
            pool.memset(zeros, 0.0).then_inc(zeroed, 1)
            pool.memset(token_of[:, :], NO_TOKEN).then_inc(no_token, 1)

            def sort_rows(u):
                pool.wait_ge(rows_kept, u * GROUP_STEPS + GROUP_STEPS)
                pool.wait_ge(slots_known[u], 1)
                if u < GROUPS:
                    pool.wait_ge(slots_cleared, 16 * GROUPS)
                for t in range(GROUP_TILES):
                    at = (u % GROUPS * GROUP_TILES + t) * D
                    pool.indirect_dma_start(
                        slots_in[u % GROUPS], bass.IndirectOffsetOnAxis(ap=slot_of[u][:, t:t + 1], axis=0),
                        normed[:, at:at + D], None).then_inc(rows_sorted[u], 16)

            def sort_tokens(u):
                pool.wait_ge(token_ready, 1)
                pool.wait_ge(tokens_cleared, 16 * GROUPS)
                for t in range(GROUP_TILES):
                    at = u % GROUPS * GROUP_TILES + t
                    pool.indirect_dma_start(
                        slot_tokens[u % GROUPS], bass.IndirectOffsetOnAxis(ap=slot_of[u][:, t:t + 1], axis=0),
                        token[:, at:at + 1], None).then_inc(tokens_sorted[u], 16)

            def fetch(g, first, end):
                pool.wait_ge(y_stored[g], 16 * SLOT_TILES)
                for t in range(first, end):
                    at = (g * GROUP_TILES + t) * D
                    pool.indirect_dma_start(
                        res[:, at:at + D], None, slots_out[g],
                        bass.IndirectOffsetOnAxis(ap=slot_of[g][:, t:t + 1], axis=0),
                        compute_op=ALU.add).then_inc(fetched[g * GROUP_STEPS + t // BATCH], 16)

            def scatter(g, first, end):
                pool.wait_ge(res_stored[g], 16 * GROUP_STEPS)
                pool.wait_ge(tokens_loaded[GROUPS + g], 16)
                for t in range(first, end):
                    pool.wait_ge(b2_added[1], t + 1)
                    pool.indirect_dma_start(
                        out, bass.IndirectOffsetOnAxis(ap=token_of[:, t:t + 1], axis=0), slot_y[:, t * D:(t + 1) * D],
                        None, bounds_check=BATCH * SEQ - 1, oob_is_err=False,
                        compute_op=ALU.add).then_inc(y_scattered, 16)

            def decay_keys(n):
                pool.wait_ge(qkv_done, BATCH * (n + 1))
                wait(pool, delta_ready, n - 1)
                pool.tensor_tensor(per_batch(kd[n % 2][:, :]),
                                   qkv[n % 2][:, :].rearrange("p (b w) -> p b w", b=BATCH)[:, :, D:2 * D],
                                   cst("decay_k").unsqueeze(1).to_broadcast([P, BATCH, D]), ALU.mult).then_inc(kd_done, 1)

            def update_carry(n):
                pool.wait_ge(delta_copied, n + 1)
                pool.tensor_tensor(per_batch(carry_new[:, :]), per_batch(carry_new[:, :]),
                                   cst("carry_mask").unsqueeze(1).to_broadcast([P, BATCH, D]),
                                   ALU.mult).then_inc(delta_masked, 1)
                pool.wait_ge(delta_masked, n + 1)
                pool.wait_ge(carry_aged, n + 1)
                pool.tensor_tensor(carry[:, :], carry[:, :], carry_new[:, :], ALU.add).then_inc(carry_done, 1)

            def outer_products(n):
                par = n % 2
                pool.wait_ge(qkv_done, BATCH * (n + 1))
                wait(pool, state_ready, PAIRS * (n - 1))
                for h in range(2):
                    if n > 0 or h > 0:
                        for b in range(BATCH):
                            last = outer_product(pool, n, h, b)
                        last.then_inc(outer_done, 1)

            sort_rows(0)
            sort_rows(1)
            fetch(0, 0, GROUP_TILES)
            share = GROUP_TILES // 4
            pool.wait_ge(slotT_ready[0], LAYER_TILES)
            pool.memset(carry[:, :], 0.0).then_inc(carry_done, 1)
            for n in range(STEPS):
                if n == 0:
                    pool.wait_ge(y_stored[1], 16 * SLOT_TILES)
                if n < 4:
                    fetch(1, n * share, (n + 1) * share)
                outer_products(n)
                if n + 1 < STEPS:
                    decay_keys(n)
                if n > 0:
                    update_carry(n - 1)
            sort_rows(2)
            sort_tokens(2)
            scatter(0, 0, EARLY_SCATTERS)
            sort_rows(3)
            sort_tokens(3)
            scatter(0, EARLY_SCATTERS, SLOT_TILES)
            scatter(1, SLOT_TILES, LAYER_TILES)

        @block.scalar
        def _(act):
            act.dma_start(const_sb[:, :], const).then_inc(const_loaded, 16)
            act.dma_start(wr_sb[:, :], wrt).then_inc(router_loaded, 16)
            act.dma_start(br_sb[:, :], br.partition_broadcast(P)).then_inc(router_loaded, 16)
            act.wait_ge(const_loaded, 16)
            nc.scalar.activation(gateT[0][:, 0:1], cst("decay_c"), ACT.Silu).then_inc(table_loaded, 1)
            act.wait_ge(x_loaded[GROUP_STEPS - 1], 16)
            act.dma_start(w1_raw, w1t).then_inc(expert_w_loaded, 16)
            act.dma_start(biases[:, :], bias.partition_broadcast(P)).then_inc(expert_w_loaded, 16)
            act.dma_start(w2_sb[:, :], w2t).then_inc(expert_w_loaded, 16)
            for dst, src in ((wqkv_sb[:, :], wqkv), (wo_sb[:, :], wo), (wg1_sb, wg1t), (wg2_sb, wg2)):
                act.dma_start(dst, src).then_inc(attn_w_loaded, 16)
            act.dma_start(gb_sb[:, 0:1], gamma).then_inc(attn_w_loaded, 16)
            act.dma_start(gb_sb[:, 1:2], beta).then_inc(attn_w_loaded, 16)
            act.dma_start(decay_sb[:, :], decay).then_inc(decay_loaded, 16)

            def normalise(dst, src, par, col, done):
                for b in range(BATCH):
                    nc.scalar.activation(dst[:, b * D:(b + 1) * D], src(b), ACT.Identity,
                                         bias=shift[par][:, col + b:col + b + 1],
                                         scale=rstd[par][:, col + b:col + b + 1]).then_inc(done, 1)

            res_tile = lambda s: lambda b: res[:, (s.n * BATCH + b) * D:(s.n * BATCH + b + 1) * D]

            def route_copy(r, par, src):
                act.wait_ge(rnT_ready, r + 1)
                wait(act, logits_ready, r - 1)
                nc.scalar.activation(rnT[par][:, :], src[:, :], ACT.Copy).then_inc(rnT_copied, 1)

            def expert_pass(l):
                def slotT_copy(t, par):
                    act.wait_ge(slotT_ready[l], t + 1)
                    wait(act, up_done[l], t - 1)
                    nc.scalar.activation(slotT_hi[par][:, :], slotT_bank[:, 0:P], ACT.Copy).then_inc(slotT_copied[l], 1)

                def relu_copy(t, par):
                    act.wait_ge(hT_ready[l], t + 1)
                    wait(act, down_done[l], t - 1)
                    nc.scalar.activation(h_T[par][:, :], hT_bank[:, :], ACT.Relu).then_inc(hT_copied[l], 1)

                k0 = ROLL_END[0] + 5
                between = ({k0: lambda: first_ahead(0), k0 + 3: lambda: first_ahead(1)} if l == 0 else {
                    1: lambda: route_copy(STEPS + 5, 1, bank[4]), 2: lambda: normalise_output(8),
                    3: lambda: output_copy(8), 4: lambda: normalise_routed(8),
                    6: lambda: route_copy(STEPS + 6, 0, bank[4]), 9: lambda: normalise_routed(9),
                    11: lambda: route_copy(STEPS + 7, 1, bank[4])})

                def copies(k, it=0):
                    if k in between:
                        between[k]()
                    if k < LAYER_TILES:
                        slotT_copy(2 * it + k, k % 2)
                    if k >= 2:
                        relu_copy(2 * it + k - 2, k % 2)

                rolled(act, copies, 0, 4 if l == 0 else 12, ROLL_END[0] if l == 0 else LAYER_TILES, LAYER_TILES + 2)

            def attn_front(s):
                act.wait_ge(xnT_ready, s.n + 1)
                wait(act, gate_ready, s.n - 1)
                nc.scalar.activation(xnT[s.par][:, :], bank[5][:, :], ACT.Copy).then_inc(xnT_copied, 1)
                if s.n >= 2:
                    age_carry(s.n - 2)
                wait(act, qS_done, PAIRS * (s.n - 1))
                wait(act, outer_done, 2 * (s.n - 1) - 1)
                if s.n == 2:
                    act.wait_ge(first_outer_done, 1)
                wait(act, kd_done, s.n - 1)
                wait(act, delta_ready, s.n - 1)
                for b in range(BATCH):
                    act.wait_ge(qkv_ready, BATCH * s.n + b + 1)
                    nc.scalar.activation(qkv[s.par][:, b * 3 * D:(b + 1) * 3 * D], bank[3 + b % 2][:, 0:3 * D],
                                         ACT.Silu).then_inc(qkv_done, 1)

            def gate_tanh(s):
                act.wait_ge(gate_ready, s.n + 1)
                wait(act, gated, s.n - 1)
                nc.scalar.activation(gateT[s.par][:, :], bank[6][:, :], ACT.Tanh, scale=0.5).then_inc(gate_done, 1)

            def normalise_output(k):
                act.wait_ge(ln_ready, ln_turn(k) + 1)
                wait(act, onT_ready, k - 1)
                normalise(o_n, lambda b: o_all[:, b * D:(b + 1) * D], k % 2, OUTPUT, on_done)

            def output_copy(k):
                act.wait_ge(onT_ready, k)
                wait(act, gated, k - 1)
                nc.scalar.activation(o_nT[:, :], bank[3][:, :], ACT.Identity, bias=gb_sb[:, 1:2],
                                     scale=gb_sb[:, 0:1]).then_inc(onT_copied, 1)

            def normalise_routed(k):
                act.wait_ge(ln_ready, ln_turn(k) + 1)
                for b in range(BATCH):
                    at, col = ((k - 2) * BATCH + b) * D, ROUTED + b
                    last = nc.scalar.activation(normed[:, at:at + D], res[:, at:at + D], ACT.Identity,
                                                bias=shift[k % 2][:, col:col + 1], scale=rstd[k % 2][:, col:col + 1])
                last.then_inc(rows_kept, 1)

            def age_carry(k):
                act.wait_ge(delta_ready, k + 1)
                act.wait_ge(carry_done, k + 1)
                act.wait_ge(inter_ready, k + 1)
                nc.scalar.activation(carry[:, :], carry[:, :], ACT.Copy, scale=cst("decay_c")).then_inc(carry_aged, 1)
                nc.scalar.activation(carry_new[:, :], bank[6][:, :], ACT.Copy).then_inc(delta_copied, 1)

            def normalise_ahead(n, par, col):
                wait(act, xnT_ready, n)
                normalise(xn, res_tile(step(n)), par, col, xn_done)

            def first_ahead(n):
                act.wait_ge(ln_ready, 1)
                normalise_ahead(n, 0, n * BATCH)

            def attention(k):
                if k + 1 < STEPS:
                    attn_front(step(k + 1))
                else:
                    age_carry(k - 1)
                if 0 <= k - 3:
                    route_copy(STEPS + k - 3, step(k - 3).par, bank[4])
                if k >= 0:
                    gate_tanh(step(k))
                    act.wait_ge(ln_ready, ln_turn(k) + 1)
                if 0 <= k - 1:
                    normalise_output(k)
                if 0 <= k - 1:
                    output_copy(k)
                if 0 <= k and k + 2 < STEPS:
                    normalise_ahead(k + 2, k % 2, AHEAD)
                if 0 <= k - 2:
                    normalise_routed(k)

            def normalise_step(r):
                for b in range(BATCH):
                    t = (r - GROUP_STEPS) * BATCH + b
                    at = slice((r * BATCH + b) * D, (r * BATCH + b + 1) * D)
                    last = nc.scalar.activation(normed[:, at], res[:, at], ACT.Identity, bias=shift[1][:, t:t + 1],
                                                scale=rstd[1][:, t:t + 1])
                last.then_inc(rows_kept, 1)

            act.wait_ge(table_loaded, 1)
            for r in range(GROUP_STEPS):
                route_copy(r, r % 2, bank[r % 2])
            act.wait_ge(ln_chain0[1], SMALL + 2)
            act.wait_ge(rows_kept, GROUP_STEPS)
            normalise_step(GROUP_STEPS)
            for r in range(GROUP_STEPS, STEPS):
                if r + 1 < STEPS:
                    normalise_step(r + 1)
                route_copy(r, r % 2, bank[r % 2])
            act.wait_ge(expert_w_loaded, 48)
            for i in range(W1_PIECES):
                w = EXPERTS * FF // W1_PIECES
                nc.scalar.activation(w1_hi[:, i * w:(i + 1) * w], w1_raw[:, i * w:(i + 1) * w], ACT.Copy).then_inc(w1_hi_done, 1)
            act.wait_ge(wg_ready, 1)
            nc.scalar.activation(wg_sb[:, :], bank[7][:, 0:D], ACT.Copy).then_inc(wg_copied, 1)
            expert_pass(0)
            act.wait_ge(attn_w_loaded, 16 * 6)
            for k in TURNS:
                attention(k)
            expert_pass(1)

        @block.vector
        def _(dve):
            def tile_stats(col, src, tiles=BATCH):
                for b in range(tiles):
                    last = nc.vector.bn_stats(st[:, col + b, :], src(b))
                return last

            def small(i, lo, hi, par, chain, base, ready):
                c = slice(lo, hi)
                stt = nc.vector.scalar_tensor_tensor
                dve.wait_ge(chain, base + i + 1)
                if i == 0:
                    nc.vector.tensor_tensor(mean2[:, c], st[:, c, 1], st[:, c, 4], ALU.add)
                    stt(out=var[:, c], in0=st[:, c, 2], scalar=D * EPS, in1=st[:, c, 5], op0=ALU.add, op1=ALU.add)
                    ins = nc.vector.tensor_tensor(tt[:, c], st[:, c, 1], st[:, c, 4], ALU.subtract)
                elif i == 1:
                    ins = nc.vector.tensor_tensor(uu[:, c], tt[:, c], tt[:, c], ALU.mult)
                elif i == 2:
                    ins = stt(out=var[:, c], in0=var[:, c], scalar=4.0 / D, in1=uu[:, c], op0=ALU.mult, op1=ALU.add)
                elif i == 3:
                    ins = nc.vector.tensor_scalar(yy[:, c].bitcast(I32), var[:, c].bitcast(I32), -0.5, RSQRT_MAGIC,
                                                  ALU.mult, ALU.add)
                elif i in (4, 7):
                    ins = nc.vector.tensor_tensor(tt[:, c], yy[:, c], yy[:, c], ALU.mult)
                elif i == 5:
                    ins = stt(out=uu[:, c], in0=tt[:, c], scalar=-0.5 / 4, in1=var[:, c], op0=ALU.mult, op1=ALU.mult)
                elif i == 6:
                    ins = stt(out=yy[:, c], in0=uu[:, c], scalar=1.5, in1=yy[:, c], op0=ALU.add, op1=ALU.mult)
                elif i == 8:
                    ins = stt(out=uu[:, c], in0=tt[:, c], scalar=ROOT_3_8 / 4, in1=var[:, c], op0=ALU.mult, op1=ALU.mult)
                elif i == 9:
                    ins = stt(out=tt[:, c], in0=uu[:, c], scalar=-10 / 8 / ROOT_3_8, in1=uu[:, c], op0=ALU.add, op1=ALU.mult)
                elif i == 10:
                    ins = stt(out=rstd[par][:, c], in0=tt[:, c], scalar=15 / 8, in1=yy[:, c], op0=ALU.add, op1=ALU.mult)
                else:
                    stt(out=shift[par][:, c], in0=mean2[:, c], scalar=-0.5, in1=rstd[par][:, c],
                        op0=ALU.mult, op1=ALU.mult).then_inc(ready, 1)
                    return
                ins.then_inc(chain, 1)

            def route_stats(g):
                for c in range(GROUP_STEPS):
                    r = g * GROUP_STEPS + c
                    dve.wait_ge(x_loaded[r], 16)
                    last = tile_stats(c * BATCH, lambda b: res[:, (r * BATCH + b) * D:(r * BATCH + b + 1) * D])
                last.then_inc(ln_chain0[g], 1)
                for i in range(SMALL + 1):
                    small(i, 0, GROUP_TILES, g, ln_chain0[g], 0, ln_chain0[g])

            def normalise_first_group():
                dve.wait_ge(ln_chain0[0], SMALL + 2)
                for t in range(GROUP_TILES):
                    ins = nc.vector.tensor_scalar(normed[:, t * D:(t + 1) * D], res[:, t * D:(t + 1) * D], rstd[0][:, t:t + 1],
                                                  shift[0][:, t:t + 1], ALU.mult, ALU.add)
                    if t % BATCH == BATCH - 1:
                        ins.then_inc(rows_kept, 1)

            def add_router_bias(at, src, tiles, added):
                n = tiles * EXPERTS
                nc.vector.tensor_tensor(
                    logits[:, bass.ds(at, n)].rearrange("p (b e) -> p b e", e=EXPERTS),
                    src[:, 0:n].rearrange("p (b e) -> p b e", e=EXPERTS),
                    br_sb[:, :].unsqueeze(1).to_broadcast([P, tiles, EXPERTS]), ALU.add).then_inc(added, 1)

            chains = [Chain(dve, route_chain[u]) for u in range(UNITS)]
            n_counts = GROUP_TILES * EXPERTS
            by_tile = lambda t: t.rearrange("p (i e) -> p i e", e=EXPERTS)
            as_tile = lambda t: t[:, :].rearrange("p (e i) -> p i e", e=EXPERTS)
            by_expert = lambda t: t[:, :].rearrange("p (e i) -> p e i", e=EXPERTS)

            def route_choose(u):
                chain, g, n = chains[u], u % GROUPS, n_counts
                if u < GROUPS:
                    dve.wait_ge(logits_added0[g], 1)
                else:
                    dve.wait_ge(logits_added, (g + 1) * GROUP_STEPS)
                spread = lambda t: t[:, :].unsqueeze(2).to_broadcast([P, GROUP_TILES, EXPERTS])
                lg, pk = by_tile(logits[:, g * n:(g + 1) * n]), by_tile(pick[:, :])
                chain.link(nc.vector.tensor_reduce(best[:, :], lg, AX_X, ALU.max))
                chain.link(nc.vector.tensor_tensor(pk, lg, spread(best), ALU.is_equal))
                chain.link(nc.vector.tensor_tensor(pk, pk, cst("prefer").unsqueeze(1).to_broadcast(
                    [P, GROUP_TILES, EXPERTS]), ALU.mult))
                chain.link(nc.vector.tensor_reduce(best[:, :], pk, AX_X, ALU.max))
                chain.link(nc.vector.tensor_tensor(as_tile(onehot), pk, spread(best), ALU.is_equal))
                nc.vector.tensor_copy(onehot_bf[:, :], onehot).then_inc(onehot_ready[u], 1)

            def route_read_counts(u):
                dve.wait_ge(counts_ready[u], 1)
                nc.vector.tensor_copy(place[:, :], counts_bank[:, 0:n_counts])
                nc.vector.tensor_copy(total[:, :], counts_bank[:, n_counts:2 * n_counts]).then_inc(counts_read[u], 1)

            def route_count(u):
                chain = chains[u]
                dve.wait_ge(counts_read[u], 1)
                chain.link(nc.vector.tensor_tensor_scan(upto[:, :], cst("not_first"), total[:, :], 0.0, ALU.mult, ALU.add))
                chain.link(nc.vector.tensor_scalar(tiles_e[:, :], by_expert(upto)[:, :, GROUP_TILES - 1], P / 2 - 0.5,
                                                   1.0 / P, ALU.add, ALU.mult))
                chain.link(nc.vector.tensor_scalar(tiles_e[:, :], tiles_e[:, :], ROUND, -ROUND, ALU.add, ALU.add))
                chain.link(nc.vector.tensor_tensor_scan(ends_e[:, :], cst("ones")[:, 0:EXPERTS], tiles_e[:, :], 0.0,
                                                        ALU.mult, ALU.add))

            def route_place(u):
                chain = chains[u]
                nc.vector.tensor_tensor(base_e[:, :], ends_e[:, :], tiles_e[:, :], ALU.subtract)
                chain.link(nc.vector.tensor_tensor(place[:, :], place[:, :], upto[:, :], ALU.add))
                chain.link(nc.vector.tensor_tensor(place[:, :], place[:, :], total[:, :], ALU.subtract))
                chain.link(nc.vector.scalar_tensor_tensor(out=by_expert(place), in0=base_e[:, :].unsqueeze(2).to_broadcast(
                    [P, EXPERTS, GROUP_TILES]), scalar=float(P), in1=by_expert(place), op0=ALU.mult, op1=ALU.add))
                chain.link(nc.vector.tensor_tensor(place[:, :], place[:, :], onehot, ALU.mult))
                chain.link(nc.vector.tensor_reduce(slot_of_f[:, :], as_tile(place), AX_X, ALU.add))
                nc.vector.tensor_copy(slot_of[u][:, :], slot_of_f[:, :]).then_inc(slots_known[u], 1)

            def route_owners(u):
                chain, g = chains[u], u % GROUPS
                ended_v = ended.rearrange("p (j e) -> p j e", e=EXPERTS)
                chain.link(nc.vector.tensor_tensor(ended_v, ends_e[0:1, :].unsqueeze(1).to_broadcast([1, SLOT_TILES, EXPERTS]),
                                                   cst("slot_tile", 1).unsqueeze(2).to_broadcast([1, SLOT_TILES, EXPERTS]),
                                                   ALU.is_le))
                chain.link(nc.vector.tensor_reduce(owner_f[:, :], ended_v, AX_X, ALU.add))
                chain.link(nc.vector.tensor_scalar(owner_f[:, :], owner_f[:, :], float(EXPERTS - 1), None, ALU.min))
                nc.vector.tensor_scalar(owner_bias[:, g * SLOT_TILES:(g + 1) * SLOT_TILES], owner_f[:, :],
                                        float(BIAS_W), None, ALU.mult)
                nc.vector.tensor_scalar(owner[:, g * SLOT_TILES:(g + 1) * SLOT_TILES], owner_f[:, :], float(FF), None,
                                        ALU.mult).then_inc(owners_known[u], 1)

            def route(u):
                for part in (route_choose, route_read_counts, route_count, route_place, route_owners):
                    part(u)

            def expert_pass(l):
                experts = Experts(dve, owner_bias, (EXPERTS - 1) * BIAS_W)

                def split(t, par):
                    dve.wait_ge(slotT_copied[l], t + 1)
                    wait(dve, up_done[l], t - 1)
                    nc.vector.tensor_tensor(slotT_lo[par][:, :], slotT_bank[:, 0:P], slotT_hi[par][:, :],
                                            ALU.subtract).then_inc(slotT_split[l], 1)

                def add_b1(t, par, e):
                    dve.wait_ge(up_done[l], t + 1)
                    wait(dve, hT_ready[l], t - 1)
                    nc.vector.tensor_tensor(h_pre[par][:, :], up_bank[:, :], biases[:, bass.ds(e, FF)],
                                            ALU.add).then_inc(b1_added[l], 1)

                def add_b2(t, par, e):
                    dve.wait_ge(down_done[l], t + 1)
                    nc.vector.scalar_tensor_tensor(out=slot_y[:, bass.ds(t * D, D)], in0=down_bank[:, 0:D], scalar=0.5,
                                                   in1=biases[:, bass.ds(e + FF, D)], op0=ALU.mult,
                                                   op1=ALU.add).then_inc(b2_added[l], 1)

                both = (OUTPUT, ROUTED + BATCH)
                if l == 0:
                    chain_at = lambda first, end: lambda: turn_small(-2, first, end, 0, 2 * BATCH)
                    k0 = ROLL_END[0]
                    between = {k0: first_stats, k0 + 1: chain_at(0, 3), k0 + 2: chain_at(3, 6), k0 + 3: chain_at(6, 9),
                               k0 + 4: chain_at(9, SMALL + 1)}
                else:
                    between = {
                        0: lambda: (output_stats(8), residual_stats(8), turn_small(8, 0, SMALL + 1, *both)),
                        2: lambda: router_bias(5), 4: lambda: gate(step(7)), 5: lambda: residual_stats(9),
                        6: lambda: (turn_small(9, 0, 6, ROUTED, ROUTED + BATCH), router_bias(6)),
                        7: lambda: turn_small(9, 6, SMALL + 1, ROUTED, ROUTED + BATCH),
                        11: lambda: (router_bias(7), route_choose(3)), 12: lambda: (route_read_counts(3), route_count(3)),
                        13: lambda: route_place(3), 14: lambda: route_owners(3)}

                def sums(k, it=0):
                    if k in between:
                        between[k]()
                    if k == 0:
                        split(0, 0)
                    if k < LAYER_TILES:
                        s = slot(k, it)
                        add_b1(s.n, s.par, experts.of(s, k))
                    if k + 1 < LAYER_TILES:
                        split(slot(k + 1, it).n, (k + 1) % 2)
                        if k + 1 not in pass_edges(l):
                            experts.of(slot(k + 1, it), k + 1)
                    if k >= 2:
                        s = slot(k - 2, it)
                        add_b2(s.n, s.par, experts.of(s, k - 2))

                dve.wait_ge(owners_known[GROUPS * l], 1)
                for k in range(ROLL_FROM):
                    sums(k)
                dve.wait_ge(owners_known[GROUPS * l + 1], 1)
                rolled(dve, sums, ROLL_FROM, ROLL_FROM, ROLL_END[l], LAYER_TILES + 2, by=ROLL,
                       edge=experts.forget)

            def front(s):
                dve.wait_ge(qT_ready, s.n + 1)
                wait(dve, inter_ready, s.n - 1)
                nc.vector.tensor_tensor(per_batch(qdT[s.par][:, :]), per_batch(bank[5][:, :]),
                                        cst("decay_q").unsqueeze(1).to_broadcast([P, BATCH, P]),
                                        ALU.mult).then_inc(qdT_done, 1)

            def times_q(s, h):
                q_ = qkv[s.par][:, :].rearrange("p (b w) -> p b w", b=BATCH)
                wait(dve, o_in_done, PAIRS * s.n + h - 2)
                dve.wait_ge(state_ready, PAIRS * s.n + h + 1)
                q2 = q_[:, :, h * 2 * HD:(h + 1) * 2 * HD].unsqueeze(3).to_broadcast([P, BATCH, 2 * HD, HD])
                nc.vector.tensor_tensor(qS[h % 3][:, :].rearrange("p (b a e) -> p b a e", b=BATCH, e=HD),
                                        bank[h % 3][:, :].rearrange("p (b a e) -> p b a e", b=BATCH, e=HD),
                                        q2, ALU.mult).then_inc(qS_done, 1)

            def sum_d(s, h):
                dve.wait_ge(qS_done, PAIRS * s.n + h + 1)
                w = BATCH * 2 * HD
                nc.vector.tensor_reduce(o_in[:, h * w:(h + 1) * w].rearrange("p (a e) -> p a e", e=HD),
                                        qS[h % 3][:, :].rearrange("p (a d e) -> p a e d", d=HD, e=HD),
                                        AX_X, ALU.add).then_inc(o_in_done, 1)

            def join(s):
                dve.wait_ge(inter_ready, s.n + 1)
                dve.wait_ge(o_in_done, PAIRS * (s.n + 1))
                wait(dve, on_done, BATCH * s.n)
                w2 = 2 * HD
                nc.vector.tensor_tensor(
                    o_all[:, :].rearrange("p (b h w) -> p b h w", b=BATCH, w=w2),
                    bank[7][:, :].rearrange("p (b h w) -> p b h w", b=BATCH, w=w2),
                    o_in[:, :].rearrange("p (h b w) -> p b h w", b=BATCH, w=w2), ALU.add).then_inc(o_done, 1)

            def gate(s):
                dve.wait_ge(onT_copied, s.n + 1)
                dve.wait_ge(gate_done, s.n + 1)
                wait(dve, wo_ready, s.n)
                nc.vector.scalar_tensor_tensor(out=o_gT[:, :], in0=gateT[s.par][:, :], scalar=1.0, in1=o_nT[:, :],
                                               op0=ALU.add, op1=ALU.mult).then_inc(gated, 1)

            def residual(s):
                dve.wait_ge(wo_ready, s.n + 1)
                nc.vector.scalar_tensor_tensor(out=of_step(res, s), in0=bank[7][:, :], scalar=0.5, in1=of_step(res, s),
                                               op0=ALU.mult, op1=ALU.add).then_inc(res_done, 1)

            res_tile = lambda s: lambda b: res[:, (s * BATCH + b) * D:(s * BATCH + b + 1) * D]

            def first_stats():
                for c in range(2):
                    dve.wait_ge(fetched[c], 16 * BATCH)
                    last = tile_stats(c * BATCH, res_tile(c))
                last.then_inc(ln_chain, 1)

            def turn_small(k, first, end, lo, hi):
                for i in range(first, end):
                    small(i, lo, hi, k % 2, ln_chain, ln_turn(k) * (SMALL + 1), ln_ready)

            def output_stats(k):
                dve.wait_ge(o_done, k)
                return tile_stats(OUTPUT, lambda b: o_all[:, b * D:(b + 1) * D])

            def residual_stats(k):
                residual(step(k - 2))
                dve.wait_ge(res_done, k - 1)
                tile_stats(ROUTED, res_tile(k - 2)).then_inc(ln_chain, 1)

            def router_bias(s):
                dve.wait_ge(logits_ready, STEPS + s + 1)
                add_router_bias(s * BATCH * EXPERTS, bank[4], BATCH, logits_added)

            def first_outer():
                dve.wait_ge(qkv_done, BATCH)
                for b in range(BATCH):
                    last = outer_product(nc.vector, 0, 0, b)
                last.then_inc(first_outer_done, 1)

            def attention(k):
                here = step(k)
                if k >= 0:
                    cols = []
                    if k + 2 < STEPS:
                        dve.wait_ge(fetched[k + 2], 16 * BATCH)
                        last = tile_stats(AHEAD, res_tile(k + 2))
                        cols.append(AHEAD)
                    if 0 <= k - 1:
                        last = output_stats(k)
                        cols.append(OUTPUT)
                    times_q(here, 0)
                    if 0 <= k - 2:
                        residual_stats(k)
                        cols.append(ROUTED)
                    else:
                        last.then_inc(ln_chain, 1)
                    lo, hi = min(cols), max(cols) + BATCH
                    for h in range(PAIRS):
                        turn_small(k, 2 * h, min(2 * h + 1, SMALL + 1), lo, hi)
                        if h + 1 < PAIRS:
                            times_q(here, h + 1)
                        turn_small(k, 2 * h + 1, min(2 * h + 2, SMALL + 1), lo, hi)
                        sum_d(here, h)
                if k == -1:
                    first_outer()
                if k + 1 < STEPS:
                    front(step(k + 1))
                if 0 <= k:
                    join(here)
                if 0 <= k - 1:
                    gate(step(k - 1))
                if 0 <= k - 3:
                    router_bias(k - 3)

            dve.wait_ge(const_loaded, 16)
            nc.vector.tensor_copy(upper_bf[:, :], cst("upper"))
            nc.vector.tensor_copy(ones_bf[:, :], cst("ones")).then_inc(bf_ready, 1)
            dve.wait_ge(router_loaded, 32)
            nc.vector.tensor_copy(token[:, :], cst("token")).then_inc(token_ready, 1)
            route_stats(0)
            normalise_first_group()
            route_stats(1)
            for g in range(GROUPS):
                dve.wait_ge(logits_ready, (g + 1) * GROUP_STEPS)
                add_router_bias(g * GROUP_TILES * EXPERTS, router_bank[g], GROUP_TILES, logits_added0[g])
                route(g)
            dve.wait_ge(expert_w_loaded, 48)
            b2_ = biases[:, :].rearrange("p (e w) -> p e w", e=EXPERTS)[:, :, FF:BIAS_W]
            nc.vector.tensor_scalar(b2_, b2_, 0.5, None, ALU.mult).then_inc(b2_halved, 1)
            dve.wait_ge(b2_halved, 1)
            for i in range(W1_PIECES):
                w = EXPERTS * FF // W1_PIECES
                dve.wait_ge(w1_hi_done, i + 1)
                nc.vector.tensor_tensor(w1_lo[:, i * w:(i + 1) * w], w1_raw[:, i * w:(i + 1) * w], w1_hi[:, i * w:(i + 1) * w],
                                        ALU.subtract).then_inc(w1_split, 1)
            dve.wait_ge(slots_cleared, 16 * GROUPS)
            expert_pass(0)
            for k in TURNS:
                attention(k)
                if k == ROUTE_TURN:
                    route(2)
            expert_pass(1)

        @block.tensor
        def _(pe):
            mm = nc.tensor.matmul

            def keep_warm(count):
                for _ in range(count):
                    mm(bank[3][:, :], ident, const_sb[:, 0:512], start=True, stop=True)

            def transpose4(dst, src, done):
                for b in range(BATCH):
                    last = nc.tensor.transpose(dst[:, b * P:(b + 1) * P], src(b), ident)
                last.then_inc(done, 1)

            def route_product(r, par, dst, at):
                pe.wait_ge(rnT_copied, r + 1)
                for b in range(BATCH):
                    last = mm(dst[:, at + b * EXPERTS:at + (b + 1) * EXPERTS], rnT[par][:, b * P:(b + 1) * P], wr_sb[:, :],
                              start=True, stop=True)
                last.then_inc(logits_ready, 1)

            def route_counts(u):
                pe.wait_ge(onehot_ready[u], 1)
                n = GROUP_TILES * EXPERTS
                mm(counts_bank[:, 0:n], upper_bf[:, :], onehot_bf[:, :], start=True, stop=True)
                mm(counts_bank[:, n:2 * n], ones_bf[:, :], onehot_bf[:, :], start=True, stop=True).then_inc(counts_ready[u], 1)

            def expert_pass(l):
                experts = Experts(pe, owner, (EXPERTS - 1) * FF)

                def slot_transpose(s):
                    pe.wait_ge(slot_loaded[l][s.buf], 16 * (s.round + 1))
                    wait(pe, slotT_split[l], s.n)
                    nc.tensor.transpose(slotT_bank[:, 0:P], slot_x[s.buf], ident).then_inc(slotT_ready[l], 1)

                def up(s, e):
                    pe.wait_ge(slotT_split[l], s.n + 1)
                    wait(pe, b1_added[l], s.n)
                    mm(up_bank[:, :], slotT_lo[s.par][:, :], w1_hi[:, bass.ds(e, FF)], start=True, stop=False)
                    mm(up_bank[:, :], slotT_hi[s.par][:, :], w1_lo[:, bass.ds(e, FF)], start=False, stop=False)
                    mm(up_bank[:, :], slotT_hi[s.par][:, :], w1_hi[:, bass.ds(e, FF)],
                       start=False, stop=True).then_inc(up_done[l], 1)

                def h_transpose(s):
                    pe.wait_ge(b1_added[l], s.n + 1)
                    wait(pe, hT_copied[l], s.n)
                    for f in range(FB):
                        last = nc.tensor.transpose(hT_bank[:, f * P:(f + 1) * P],
                                                   h_pre[s.par][:, f * P:(f + 1) * P], ident)
                    last.then_inc(hT_ready[l], 1)

                def down(s, e):
                    pe.wait_ge(hT_copied[l], s.n + 1)
                    wait(pe, b2_added[l], s.n)
                    for f in range(FB):
                        last = mm(down_bank[:, 0:D], h_T[s.par][:, f * P:(f + 1) * P],
                                  w2_sb[:, bass.ds(e + f * D, D)], start=(f == 0), stop=(f == FB - 1))
                    last.then_inc(down_done[l], 1)

                def stages(k, it=0):
                    if 0 <= k < LAYER_TILES:
                        up(slot(k, it), experts.of(slot(k, it), k))
                    if 0 <= k - 2:
                        e_down = experts.of(slot(k - 2, it), k - 2)
                    if k + 1 < LAYER_TILES:
                        slot_transpose(slot(k + 1, it))
                    if 0 <= k - 1 < LAYER_TILES:
                        h_transpose(slot(k - 1, it))
                    if k + 1 < LAYER_TILES and k + 1 not in pass_edges(l):
                        experts.of(slot(k + 1, it), k + 1)
                    if 0 <= k - 2:
                        down(slot(k - 2, it), e_down)
                    if k in between:
                        between[k]()

                route = lambda s: route_product(STEPS + s, s % 2, bank[4], 0)
                between = {ROLL_END[0] + 6: lambda: norm_transpose(step(0))} if l == 0 else {
                    0: lambda: route(5),
                    2: lambda: out_transpose(step(7)), 4: lambda: (out_product(step(7)), route_transpose(step(6))),
                    5: lambda: route(6), 9: lambda: route_transpose(step(7)), 10: lambda: route(7),
                    11: lambda: route_counts(3)}
                if l == 1:
                    out_product(step(6))
                    route_transpose(step(5))
                    keep_warm(WARM_EXPERTS[1])
                    pe.wait_ge(qS_done, STEPS * PAIRS)
                pe.wait_ge(owners_known[GROUPS * l], 1)
                for k in range(-1, ROLL_FROM):
                    stages(k)
                pe.wait_ge(owners_known[GROUPS * l + 1], 1)
                rolled(pe, stages, ROLL_FROM, ROLL_FROM, ROLL_END[l], LAYER_TILES + 2, by=ROLL, edge=experts.forget)

            def norm_transpose(s):
                pe.wait_ge(xn_done, BATCH * (s.n + 1))
                wait(pe, qdT_done, s.n)
                transpose4(bank[5], lambda b: xn[:, b * D:(b + 1) * D], xnT_ready)

            def project(s, b):
                pe.wait_ge(xnT_copied, s.n + 1)
                wait(pe, qkv_done, BATCH * s.n + b - 1)
                if b == 0:
                    wait(pe, onT_copied, s.n - 2)
                if b == 1:
                    wait(pe, logits_added, s.n - 4)
                mm(bank[3 + b % 2][:, 0:3 * D], xnT[s.par][:, b * P:(b + 1) * P], wqkv_sb[:, :],
                   start=True, stop=True).then_inc(qkv_ready, 1)

            def gate_product(s):
                if s.n == 0:
                    pe.wait_ge(b2_added[0], LAYER_TILES)
                wait(pe, delta_copied, s.n)
                mm(bank[6][:, :], wg_sb[:, :], xnT[s.par][:, :], start=True, stop=True).then_inc(gate_ready, 1)

            def state_product(s, h):
                if s.n == 0 and h == 0:
                    pe.wait_ge(first_outer_done, 1)
                if s.n > 0 or h >= PAIRS // 2:
                    pe.wait_ge(outer_done, 2 * s.n + h // (PAIRS // 2))
                before = PAIRS * s.n + h - 3 if h >= 3 else PAIRS * (s.n - 1) + 6 + h if h < 2 else PAIRS * (s.n - 1) + 5
                wait(pe, qS_done, before + 1)
                for a in range(2):
                    u = outer[s.par][:, :].rearrange("p (b w) -> p b w", b=BATCH)[:, :, (2 * h + a) * UH:(2 * h + a + 1) * UH]
                    to = bank[h % 3][:, :].rearrange("p (b a w) -> p b a w", b=BATCH, a=2)[:, :, a, :]
                    last = mm(to, decay_sb[:, (2 * h + a) * P:(2 * h + a + 1) * P], u, start=True, stop=True)
                last.then_inc(state_ready, 1)

            def inter_product(s):
                pe.wait_ge(qdT_done, s.n + 1)
                pe.wait_ge(carry_done, s.n + 1)
                wait(pe, res_done, s.n - 1)
                for b in range(BATCH):
                    last = mm(bank[7][:, b * D:(b + 1) * D], qdT[s.par][:, b * P:(b + 1) * P], carry[:, b * D:(b + 1) * D],
                              start=True, stop=True)
                last.then_inc(inter_ready, 1)

            def carry_product(s):
                pe.wait_ge(kd_done, s.n + 1)
                pe.wait_ge(gate_done, s.n + 1)
                for b in range(BATCH):
                    v_ = qkv[s.par][:, b * 3 * D + 2 * D:(b + 1) * 3 * D]
                    last = mm(bank[6][:, b * D:(b + 1) * D], kd[s.par][:, b * D:(b + 1) * D], v_, start=True, stop=True)
                last.then_inc(delta_ready, 1)

            def q_transpose(s):
                pe.wait_ge(qkv_done, BATCH * (s.n + 1))
                transpose4(bank[5], lambda b: qkv[s.par][:, b * 3 * D:b * 3 * D + D], qT_ready)

            def out_transpose(s):
                pe.wait_ge(on_done, BATCH * (s.n + 1))
                wait(pe, onT_copied, s.n)
                transpose4(bank[3], lambda b: o_n[:, b * D:(b + 1) * D], onT_ready)

            def out_product(s):
                pe.wait_ge(gated, s.n + 1)
                pe.wait_ge(o_done, min(s.n + 2, STEPS))
                for b in range(BATCH):
                    last = mm(bank[7][:, b * D:(b + 1) * D], o_gT[:, b * P:(b + 1) * P], wo_sb[:, :], start=True, stop=True)
                last.then_inc(wo_ready, 1)

            def route_transpose(s):
                pe.wait_ge(rows_kept, STEPS + s.n + 1)
                wait(pe, logits_added, s.n)
                transpose4(bank[4], lambda b: normed[:, (s.n * BATCH + b) * D:(s.n * BATCH + b + 1) * D], rnT_ready)

            def attention(k):
                cur, nxt = step(k), step(k + 1)
                has_cur, has_nxt = 0 <= k < STEPS, 0 <= k + 1 < STEPS
                for h in range(PAIRS):
                    if has_cur:
                        state_product(cur, h)
                    if h == 0 and 0 <= k - 2 < STEPS:
                        out_product(step(k - 2))
                    if has_nxt:
                        if h == 0 and k >= 0:
                            norm_transpose(nxt)
                        if 1 <= h <= BATCH:
                            project(nxt, h - 1)
                        if h == BATCH + 2:
                            q_transpose(nxt)
                    if has_cur and h == BATCH + 1:
                        gate_product(cur)
                    if 0 <= k - 3 and h == BATCH + 2:
                        route_transpose(step(k - 3))
                if has_cur:
                    inter_product(cur)
                    if k + 1 < STEPS:
                        carry_product(cur)
                if 0 <= k - 1 < STEPS:
                    out_transpose(step(k - 1))
                if 0 <= k - 3:
                    s = step(k - 3)
                    route_product(STEPS + s.n, s.par, bank[4], 0)

            pe.wait_ge(const_loaded, 16)
            keep_warm(WARM_ROUTING)
            pe.wait_ge(router_loaded, 32)
            for g in range(GROUPS):
                for k in range(GROUP_STEPS + 1):
                    r = g * GROUP_STEPS + k
                    if k < GROUP_STEPS:
                        pe.wait_ge(rows_kept, r + 1)
                        wait(pe, rnT_copied, r - 1)
                        transpose4(bank[r % 2], lambda b: normed[:, (r * BATCH + b) * D:(r * BATCH + b + 1) * D], rnT_ready)
                    if k >= 1:
                        route_product(r - 1, (r - 1) % 2, router_bank[g], (k - 1) * BATCH * EXPERTS)
                if g == 0:
                    pe.wait_ge(bf_ready, 1)
                    route_counts(0)
            pe.wait_ge(counts_read[0], 1)
            route_counts(1)
            pe.wait_ge(attn_w_loaded, 16 * 6)
            mm(bank[7][:, 0:D], wg1_sb, wg2_sb, start=True, stop=True).then_inc(wg_ready, 1)
            pe.wait_ge(expert_w_loaded, 48)
            pe.wait_ge(wg_copied, 1)
            pe.wait_ge(rows_sorted[0], 16 * GROUP_TILES)
            keep_warm(WARM_EXPERTS[0])
            pe.wait_ge(w1_split, W1_PIECES)
            expert_pass(0)
            pe.wait_ge(decay_loaded, 16)
            for k in TURNS:
                attention(k)
                if k == ROUTE_TURN:
                    pe.wait_ge(qdT_done, k + 2)
                    route_counts(2)
                    pe.wait_ge(counts_read[2], 1)
            expert_pass(1)


def head_slopes():
    start = 2.0 ** (-2.0 ** (-(np.log2(HEADS) - 3)))
    s = np.array([start * start ** i for i in range(HEADS)], dtype=np.float32)
    return (s * np.float32(1.0 + 1e-05)).astype(np.float64)


def constants():
    s, i = head_slopes(), np.arange(P, dtype=np.float64)
    diff = i[None, :] - i[:, None]
    decay = np.where(diff >= 0, np.exp(-s[:, None, None] * np.maximum(diff, 0)), 0.0)
    per_row = np.repeat(s, HD)
    head = np.arange(P) // HD
    parts = {
        "ident": np.eye(P),
        "carry_mask": head[:, None] == head[None, :],
        "decay_q": np.exp(-per_row[:, None] * (i[None, :] + 1)),
        "decay_k": np.exp(-per_row[None, :] * (P - 1 - i[:, None])),
        "decay_c": np.exp(-per_row[:, None] * P),
        "upper": diff > 0,
        "ones": np.ones((P, P)),
        "not_first": np.tile((np.arange(EXPERTS * GROUP_TILES) % GROUP_TILES != 0)[None, :], (P, 1)),
        "prefer": np.tile((EXPERTS - np.arange(EXPERTS))[None, :], (P, 1)),
        "token": i[:, None] + P * (np.arange(STEPS)[:, None] + STEPS * np.arange(BATCH)[None, :]).reshape(1, -1),
        "slot_tile": np.tile(np.arange(SLOT_TILES)[None, :], (P, 1)),
    }
    const = np.concatenate([np.asarray(parts[n], dtype=np.float64) for n in CONST], axis=1).astype(np.float32)
    return decay.transpose(1, 0, 2).reshape(P, HEADS * P).astype(np.float32), const


def kernel(**inputs):
    import concourse.bacc as bacc
    from concourse.bass_utils import run_bass_kernel_spmd

    a = {k: np.asarray(v) for k, v in inputs.items()}
    decay, const = constants()
    w2 = a["L0_ffn_W2"].reshape(EXPERTS, D, FB, P)
    arrays = {
        "x": a["L0_attn_x"].reshape(BATCH * SEQ, D),
        "w1t": a["L0_ffn_W1"].transpose(2, 0, 1).reshape(D, EXPERTS * FF),
        "bias": np.concatenate([a["L0_ffn_b1"], a["L0_ffn_b2"]], axis=1).reshape(EXPERTS * BIAS_W),
        "w2t": w2.transpose(3, 0, 2, 1).reshape(P, EXPERTS * FB * D),
        "wrt": a["L0_ffn_Wr"].T,
        "br": a["L0_ffn_br"],
        "wqkv": np.concatenate([a["L0_attn_Wq"], a["L0_attn_Wk"], a["L0_attn_Wv"]], axis=1),
        "wg1t": a["L0_attn_Wg1"].T,
        "wg2": a["L0_attn_Wg2"],
        "wo": a["L0_attn_Wo"],
        "gamma": a["L0_attn_gamma"].reshape(D, 1),
        "beta": a["L0_attn_beta"].reshape(D, 1),
        "decay": decay,
        "const": const,
    }
    nc = bacc.Bacc("TRN2", target_bir_lowering=False, num_devices=1)
    arrays = {f"in_{k}": np.ascontiguousarray(v) for k, v in arrays.items()}
    args = [nc.dram_tensor(k, v.shape, mybir.dt.from_np(v.dtype), kind="ExternalInput").ap() for k, v in arrays.items()]
    out = nc.dram_tensor("out_x", (BATCH * SEQ, D), F32, kind="ExternalOutput").ap()
    build(nc, *args, out)
    r = run_bass_kernel_spmd(nc, [arrays], core_ids=[0])
    return r.results[0]["out_x"].reshape(BATCH, SEQ, D)
```
